# Optimizing a Trainium2 kernel written in Bass

```python
import numpy as np
import jax
import jax.numpy as jnp

def _softmax(x, axis=-1):
    return jax.nn.softmax(x, axis=axis)

def _gelu(x):
    return jax.nn.gelu(x, approximate=True)

def _silu(x):
    return jax.nn.silu(x)

def _sigmoid(x):
    return jax.nn.sigmoid(x)

def _layernorm(x, axis=-1, eps=1e-05):
    m = jnp.mean(x, axis=axis, keepdims=True)
    v = jnp.var(x, axis=axis, keepdims=True)
    return (x - m) / jnp.sqrt(v + eps)

def _scatter_add(tgt, idx, src, axis=0):
    return tgt.at[idx].add(src)

def _segment_sum(src, seg, n):
    return jax.ops.segment_sum(src, seg, n)
kernel_name = 'mk_hybrid_d1_jaxref_r4_d09ad8'

def setup_inputs(seed: int=0):
    np.random.seed(seed)
    _w = jnp.asarray

    def _L0_attn_a_setup():
        import jax, jax.numpy as jnp
        import numpy as np
        HEADS = 32
        key = jax.random.key(seed)
        ks = jax.random.split(key, 5)
        H = 1024
        B, S = (2, 512)
        w_scale = 1.0 / np.sqrt(H)
        return {'x': jax.random.normal(ks[0], (B, S, H), dtype=jnp.float32), 'attn_qkvw': jax.random.normal(ks[1], (H, 3 * H), dtype=jnp.float32) * w_scale, 'attn_qkvb': jax.random.normal(ks[2], (3 * H,), dtype=jnp.float32) * 0.02, 'attn_ow': jax.random.normal(ks[3], (H, H), dtype=jnp.float32) * w_scale, 'attn_ob': jax.random.normal(ks[4], (H,), dtype=jnp.float32) * 0.02}
    _L0_attn_a_in = _L0_attn_a_setup()

    def _L0_attn_b_setup():
        import jax, jax.numpy as jnp
        import numpy as np
        HDC_DIM = 1024
        N_HEADS = 4
        HEAD_DIM = HDC_DIM // N_HEADS

        def _ste_sign(w):
            alpha = jnp.mean(jnp.abs(w), axis=-1, keepdims=True)
            hard = alpha * jnp.sign(w)
            hard = jnp.where(hard == 0, alpha, hard)
            return jax.lax.stop_gradient(hard - w) + w
        key = jax.random.key(seed)
        kx, kq, kk, kv = jax.random.split(key, 4)
        B, T = (4, 512)
        x = jax.random.normal(kx, (B, T, HDC_DIM), dtype=jnp.float32)
        bv_q = jax.random.normal(kq, (N_HEADS, HEAD_DIM), dtype=jnp.float32) * 0.02
        bv_k = jax.random.normal(kk, (N_HEADS, HEAD_DIM), dtype=jnp.float32) * 0.02
        bv_v = jax.random.normal(kv, (N_HEADS, HEAD_DIM), dtype=jnp.float32) * 0.02
        return {'x': x, 'bv_q': bv_q, 'bv_k': bv_k, 'bv_v': bv_v}
    _L0_attn_b_in = _L0_attn_b_setup()

    def _L0_ffn_setup():
        import jax, jax.numpy as jnp
        import numpy as np
        IN_F = 1024
        OUT_F = 1024
        N_CLUSTERS = 64
        THRESHOLD = 0.01
        TEMPERATURE = 0.1
        BATCH, SEQ = (4, 512)
        key = jax.random.key(seed)
        k1, k2, k3, k4, k5 = jax.random.split(key, 5)
        s = 1.0 / np.sqrt(IN_F)
        return {'input': jax.random.normal(k1, (BATCH, SEQ, IN_F), dtype=jnp.float32), 'weight': jax.random.normal(k2, (OUT_F, IN_F), dtype=jnp.float32) * s, 'bias': jax.random.uniform(k3, (OUT_F,), dtype=jnp.float32, minval=-s, maxval=s), 'centroids': jax.random.normal(k4, (N_CLUSTERS, IN_F), dtype=jnp.float32) * s, 'assignments': jax.random.randint(k5, (OUT_F,), 0, N_CLUSTERS, dtype=jnp.int32)}
    _L0_ffn_in = _L0_ffn_setup()
    _d = {'L0_attn_a_x': _L0_attn_a_in['x'], 'L0_attn_a_attn_qkvw': _L0_attn_a_in['attn_qkvw'], 'L0_attn_a_attn_qkvb': _L0_attn_a_in['attn_qkvb'], 'L0_attn_a_attn_ow': _L0_attn_a_in['attn_ow'], 'L0_attn_a_attn_ob': _L0_attn_a_in['attn_ob'], 'L0_attn_b_bv_q': _L0_attn_b_in['bv_q'], 'L0_attn_b_bv_k': _L0_attn_b_in['bv_k'], 'L0_attn_b_bv_v': _L0_attn_b_in['bv_v'], 'L0_ffn_weight': _L0_ffn_in['weight'], 'L0_ffn_bias': _L0_ffn_in['bias'], 'L0_ffn_centroids': _L0_ffn_in['centroids'], 'L0_ffn_assignments': _L0_ffn_in['assignments']}
    _x0 = _d['L0_attn_a_x']
    _d['L0_attn_a_x'] = jax.random.normal(jax.random.fold_in(jax.random.key(seed), 1), (8, 512, 1024), dtype=_x0.dtype)
    del _x0
    return _d

def reference(L0_attn_a_x, L0_attn_a_attn_qkvw, L0_attn_a_attn_qkvb, L0_attn_a_attn_ow, L0_attn_a_attn_ob, L0_attn_b_bv_q, L0_attn_b_bv_k, L0_attn_b_bv_v, L0_ffn_weight, L0_ffn_bias, L0_ffn_centroids, L0_ffn_assignments):

    def _L0_attn_a_ref(x, attn_qkvw, attn_qkvb, attn_ow, attn_ob):
        import jax, jax.numpy as jnp
        import numpy as np
        HEADS = 32
        B, S, H = x.shape
        hd = H // HEADS
        scale = 1.0 / np.sqrt(hd)
        qkv = x @ attn_qkvw + attn_qkvb
        qkv = qkv.reshape(B, S, 3, HEADS, hd)
        q = jnp.transpose(qkv[:, :, 0], (0, 2, 1, 3))
        k = jnp.transpose(qkv[:, :, 1], (0, 2, 1, 3))
        v = jnp.transpose(qkv[:, :, 2], (0, 2, 1, 3))
        scores = jnp.einsum('bhqd,bhkd->bhqk', q, k) * scale
        probs = jax.nn.softmax(scores, axis=-1)
        ctx = jnp.einsum('bhqk,bhkd->bhqd', probs, v)
        ctx = jnp.transpose(ctx, (0, 2, 1, 3)).reshape(B, S, H)
        return ctx @ attn_ow + attn_ob

    def _L0_attn_b_ref(x, bv_q, bv_k, bv_v):
        import jax, jax.numpy as jnp
        import numpy as np
        HDC_DIM = 1024
        N_HEADS = 4
        HEAD_DIM = HDC_DIM // N_HEADS

        def _ste_sign(w):
            alpha = jnp.mean(jnp.abs(w), axis=-1, keepdims=True)
            hard = alpha * jnp.sign(w)
            hard = jnp.where(hard == 0, alpha, hard)
            return jax.lax.stop_gradient(hard - w) + w
        B, T, D = x.shape
        H, HD = (N_HEADS, HEAD_DIM)
        scale = HD ** (-0.5)
        q_bind = _ste_sign(bv_q)
        k_bind = _ste_sign(bv_k)
        v_bind = _ste_sign(bv_v)
        xh = x.reshape(B, T, H, HD)
        Q = xh * q_bind
        K = xh * k_bind
        V = xh * v_bind
        scores = jnp.einsum('bthd,bshd->bhts', Q, K) * scale
        causal = jnp.tril(jnp.ones((T, T), dtype=bool))
        attn = jnp.where(causal, jax.nn.sigmoid(scores * 4.0), 0.0)
        out = jnp.einsum('bhts,bshd->bthd', attn, V)
        return out.reshape(B, T, D)

    def _L0_ffn_ref(input, weight, bias, centroids, assignments):
        import jax, jax.numpy as jnp
        import numpy as np
        IN_F = 1024
        OUT_F = 1024
        N_CLUSTERS = 64
        THRESHOLD = 0.01
        TEMPERATURE = 0.1
        BATCH, SEQ = (4, 512)
        shape = input.shape
        x = input.reshape(-1, shape[-1])
        dots = jax.nn.softmax(x @ centroids.T / TEMPERATURE, axis=-1)
        hits = dots > THRESHOLD
        query_sel = jnp.any(hits, axis=1)
        cluster_sel = jnp.any(hits, axis=0)
        row_sel = cluster_sel[assignments]
        dense = x @ weight.T + bias
        out = jnp.where(query_sel[:, None] & row_sel[None, :], dense, jnp.zeros((), dense.dtype))
        return out.reshape(*shape[:-1], -1)
    x = L0_attn_a_x
    x = x + _L0_attn_a_ref(_layernorm(x, axis=-1), L0_attn_a_attn_qkvw, L0_attn_a_attn_qkvb, L0_attn_a_attn_ow, L0_attn_a_attn_ob)
    x = x + _L0_ffn_ref(_layernorm(x, axis=-1), L0_ffn_weight, L0_ffn_bias, L0_ffn_centroids, L0_ffn_assignments)
    x = x + _L0_attn_b_ref(_layernorm(x, axis=-1), L0_attn_b_bv_q, L0_attn_b_bv_k, L0_attn_b_bv_v)
    x = x + _L0_ffn_ref(_layernorm(x, axis=-1), L0_ffn_weight, L0_ffn_bias, L0_ffn_centroids, L0_ffn_assignments)
    return x

_drawn_inputs = setup_inputs


def setup_inputs(seed=0):
    import zlib

    import numpy as np

    out = dict(_drawn_inputs(seed))
    spreads = {}
    factors = {'L0_attn_b_bv_q': 64.0, 'L0_attn_b_bv_k': 64.0}
    for name, (base, spread) in spreads.items():
        noise = np.random.default_rng([zlib.crc32(name.encode()), seed]).standard_normal(out[name].shape)
        drawn = base * np.exp(spread * noise) if base else spread * noise
        out[name] = jnp.asarray(drawn.astype(out[name].dtype))
    for name, factor in factors.items():
        out[name] = (out[name] * factor).astype(out[name].dtype)
    return out
```

```python
from contextlib import ExitStack

import concourse.bass as bass
from concourse import mybir

P = 128
ALU = mybir.AluOpType
ACT = mybir.ActivationFunctionType
AX = mybir.AxisListType
F32 = mybir.dt.float32
F16 = mybir.dt.float16
I32 = mybir.dt.int32
RMAX = bass.bass_isa.ReduceOp.max

HEADS_A = 32
HEADS_B = 4
LN_EPS = 1e-5
HIT = 0.01
TEMPERATURE = 0.1
EXP_MASK = 0x7F800000
EXP_TWICE = 0x7F000000
ONES_ROW = 16384.0
GH = 4
NC = 64
RING = 8


def wait(eng, sem, value):
    if not (isinstance(value, int) and value <= 0):
        eng.wait_ge(sem, value)


def wait_apart(eng, sem, value):
    if isinstance(value, int):
        wait(eng, sem, value)
    else:
        value = eng.to_reg(value)
        eng.wait_ge(sem, 1)
        eng.wait_ge(sem, value)


def scale_from_absmax(dve, m, e, s, done, n):
    dve.tensor_scalar(m, m, 1e-30, 8e37, ALU.max, ALU.min).then_inc(done, 1)
    dve.wait_ge(done, n + 1)
    dve.tensor_single_scalar(e.bitcast(I32), m.bitcast(I32), EXP_MASK, ALU.bitwise_and).then_inc(done, 1)
    dve.wait_ge(done, n + 2)
    dve.tensor_scalar(s.bitcast(I32), e.bitcast(I32), -1.0, float(EXP_TWICE), ALU.mult, ALU.add).then_inc(done, 1)
    dve.wait_ge(done, n + 3)
    return n + 3


class LnTiles:

    def __init__(self, sb, stack, n):
        self.st6 = sb(stack, "st6" + n, [P, 2, 2, 6])
        self.mv = sb(stack, "mv" + n, [P, 2, 2])
        self.rstd = sb(stack, "rstd" + n, [P, 2])


class HitTiles(LnTiles):

    def __init__(self, sb, stack, n):
        super().__init__(sb, stack, n)
        self.xT = sb(stack, "xT" + n, [P, 2, 2, 8, P], F16)
        self.nm = sb(stack, "nm" + n, [P, 2])
        self.bias = sb(stack, "bias" + n, [P, 2])
        self.e = sb(stack, "e" + n, [P, 2, NC])
        self.sum = sb(stack, "sum" + n, [P, 2])
        self.thr = sb(stack, "thr" + n, [P, 2])
        self.hit = sb(stack, "hit" + n, [P, 2, NC])


class LnSems:

    def __init__(self, sem, n):
        self.stat, self.aggr, self.var, self.rstd, self.xn = (sem(f"{a}{n}") for a in ("stat", "aggr", "var", "rstd", "xn"))


class HitSems(LnSems):

    def __init__(self, sem, n):
        super().__init__(sem, n)
        self.turned, self.hi, self.lo, self.logits, self.nmax, self.bias, self.exp, self.thr, self.hit, self.acc = (
            sem(f"hit_{a}{n}") for a in ("turned", "hi", "lo", "logits", "nmax", "bias", "exp", "thr", "hit", "acc"))


def hit_stats(dve, hs, t, x, n, par):
    for i in range(2):
        dve.bn_stats(t.st6[:, par, i, :], x[:, 512 * i:512 * i + 512]).then_inc(hs.stat, 1)
    wait_apart(dve, hs.stat, 2 * n + 2)
    dve.bn_aggr(t.mv[:, par], t.st6[:, par].rearrange("p a b -> p (a b)")).then_inc(hs.aggr, 1)


def hit_norm(pool, nc, hs, t, x, xn, mhalf, n, par):
    wait_apart(pool, hs.aggr, n + 1)
    r = t.rstd[:, par:par + 1]
    nc.gpsimd.tensor_scalar(r, t.mv[:, par, 1:2], LN_EPS, None, ALU.add).then_inc(hs.var, 1)
    pool.wait_ge(hs.var, n + 1)
    nc.gpsimd.tensor_tensor(r, r, mhalf[:], ALU.pow).then_inc(hs.rstd, 1)
    wait_apart(pool, hs.rstd, n + 1)
    nc.gpsimd.tensor_scalar(xn, x, t.mv[:, par, 0:1], r, ALU.subtract, ALU.mult).then_inc(hs.xn, 1)


def hit_turn(pe, hs, t, x_ps, xn, ident, n, par):
    pe.wait_ge(hs.xn, n + 1)
    for half in range(2):
        wait(pe, hs.lo, 2 * n - 1 + half if not isinstance(n, int) or n > 0 else 0)
        for c in range(4):
            h0 = P * (4 * half + c)
            mm = pe.transpose(x_ps[:, half, P * c:P * c + P], xn[:, h0:h0 + P], ident[:])
        mm.then_inc(hs.turned, 1)


def hit_hi(act, nc, hs, t, x_ps, n, par, stored, k, b):
    wait(act, hs.logits, n - 1)
    wait(act, stored[(k - 2) % len(stored)], 32 * (b + (k - 2) // len(stored) + 1) if not isinstance(n, int) or n > 1 else 0)
    for half in range(2):
        act.wait_ge(hs.turned, 2 * n + half + 1)
        nc.scalar.activation(t.xT[:, par, 0, 4 * half:4 * half + 4, :],
                             x_ps[:, half, :].rearrange("p (c n) -> p c n", c=4), ACT.Copy).then_inc(hs.hi, 1)


def hit_lo(dve, hs, t, x_ps, n, par):
    for half in range(2):
        dve.wait_ge(hs.hi, 2 * n + half + 1)
        dve.tensor_tensor(t.xT[:, par, 1, 4 * half:4 * half + 4, :], x_ps[:, half, :].rearrange("p (c n) -> p c n", c=4),
                          t.xT[:, par, 0, 4 * half:4 * half + 4, :], ALU.subtract).then_inc(hs.lo, 1)


def hit_logits(pe, hs, t, c_ps, centT, n, par):
    pe.wait_ge(hs.lo, 2 * n + 2)
    wait(pe, hs.exp, n)
    for i in range(24):
        c, (xp, wp) = i // 3, ((0, 0), (0, 1), (1, 0))[i % 3]
        mm = pe.matmul(c_ps[:, 0:NC], t.xT[:, par, xp, c, :], centT[:, wp, c, :], start=(i == 0), stop=(i == 23))
    mm.then_inc(hs.logits, 1)


def hit_exp(act, nc, hs, t, c_ps, cent_scale, n, par):
    act.wait_ge(hs.bias, n + 1)
    nc.scalar.activation(t.e[:, par], c_ps[:, 0:NC], ACT.Exp, bias=t.bias[:, par:par + 1], scale=cent_scale[:, 0:1],
                         accum_out=t.sum[:, par:par + 1]).then_inc(hs.exp, 1)


def hit_select(dve, hs, t, c_ps, cent_scale, hits, qsel, n, par):
    one = slice(par, par + 1)
    dve.wait_ge(hs.logits, n + 1)
    dve.tensor_reduce(t.nm[:, one], c_ps[:, 0:NC], AX.X, ALU.max, negate=True).then_inc(hs.nmax, 1)
    dve.wait_ge(hs.nmax, n + 1)
    dve.tensor_scalar(t.bias[:, one], t.nm[:, one], cent_scale[:, 0:1], None, ALU.mult).then_inc(hs.bias, 1)
    dve.wait_ge(hs.exp, n + 1)
    dve.tensor_scalar(t.thr[:, one], t.sum[:, one], HIT, None, ALU.mult).then_inc(hs.thr, 1)
    dve.wait_ge(hs.thr, n + 1)
    dve.tensor_scalar(t.hit[:, par], t.e[:, par], t.thr[:, one], None, ALU.is_gt).then_inc(hs.hit, 1)
    dve.wait_ge(hs.hit, n + 1)
    dve.tensor_reduce(qsel[:, bass.ds(n, 1)], t.hit[:, par], AX.X, ALU.max)
    dve.tensor_tensor(hits, hits, t.hit[:, par], ALU.max).then_inc(hs.acc, 1)


def hybrid_layer(nc, x, qkvw, qkvb, ow, ob, bvq, bvk, bvv, fw, fb, cent, assign, out):
    B, S, H = x.shape
    C = H // P
    T = S // P
    HD = H // HEADS_A
    G = HEADS_A // GH
    assert HD * GH == P and S == 512 and H == 1024 and G == 8 and T == 4
    TOT = B * HEADS_A
    V1 = 2 * HD + 1

    ctx_d = nc.dram_tensor("ctx_scratch", (B * G, T, P, P), F32).ap()

    x1_d = nc.dram_tensor("x1_scratch", (B * T, P, H), F32).ap()
    x3_d = nc.dram_tensor("x3_scratch", (B * T, P, H), F32).ap()
    wT_d = nc.dram_tensor("wT_scratch", (P, 2, C, H), F16).ap()
    xT1_d = nc.dram_tensor("xT1_scratch", (B * T, P, 2, C, P), F16).ap()
    xT3_d = nc.dram_tensor("xT3_scratch", (B * T, P, 2, C, P), F16).ap()

    x_t = x.rearrange("b (t p) h -> b t p h", p=P)
    out_t = out.rearrange("b (t p) h -> (b t) p h", p=P)
    ctx_t = ctx_d.rearrange("(b g) t p d -> b g t p d", g=G)

    with ExitStack() as top:
        phase_sems = []

        def sem(name):
            phase_sems.append(nc.alloc_semaphore(name=name))
            return phase_sems[-1]

        def end_phase():
            nc.clear_and_free_semaphores(list(phase_sems))
            phase_sems.clear()
            nc.all_engine_barrier()

        def sb(stack, name, shape, dt=F32):
            return stack.enter_context(nc.sbuf_tensor(name, shape, dt))

        def ps(stack, name, shape):
            return stack.enter_context(nc.psum_tensor(name, shape, F32))

        ident = sb(top, "ident", [P, P])
        e_v = sb(top, "e_v", [P, 1])
        s_v = sb(top, "s_v", [P, 1])

        with ExitStack() as p01:
            wqk = sb(p01, "wqk", [P, 2, C, 2 * H], F16)
            wv = sb(p01, "wv", [P, 2, C, H], F16)
            bqk = sb(p01, "bqk", [P, 2 * H // P])
            exp_scale = sb(p01, "exp_scale", [P, 1])

            with ExitStack() as p0:
                stg = sb(p0, "stg", [P, C, 2 * H])
                stgv = sb(p0, "stgv", [P, C, H])
                mx = sb(p0, "mx", [P, 2, C + 1])
                bias = sb(p0, "bias", [P, 3 * H // P])
                m1 = sb(p0, "m1", [P, 2])
                m2 = sb(p0, "m2", [P, 2])
                es = sb(p0, "es", [P, 2])
                sc = sb(p0, "sc", [P, 2])
                qk_in, v_in, b_in = sem("qk_in"), sem("v_in"), sem("b_in")
                p0_max, p0_all, p0_sc, p0_hi, p0_id = (sem(n) for n in ("p0_max", "p0_all", "p0_sc", "p0_hi", "p0_id"))
                in_c = [sem(f"wc_in{c}") for c in range(C)]
                with nc.Block() as block:
                    @block.sync
                    def _(sp):
                        w_c = qkvw.rearrange("(c p) n -> c p n", p=P)
                        for c in range(C):
                            sp.dma_start(stg[:, c, :], w_c[c, :, 0:2 * H]).then_inc(in_c[c], 16)
                        for c in range(C):
                            sp.dma_start(stgv[:, c, :], w_c[c, :, 2 * H:3 * H]).then_inc(v_in, 16)

                    @block.gpsimd
                    def _(pool):
                        with nc.allow_non_contiguous_dma(reason="a small bias, one feature per partition"):
                            pool.dma_start(bias[:], qkvb.rearrange("(c p) -> p c", p=P)).then_inc(b_in, 16)
                        nc.gpsimd.memset(ident[:], 0.0).then_inc(p0_id, 1)
                        pool.wait_ge(p0_id, 1)
                        nc.gpsimd.affine_select(out=ident[:], in_=ident[:], compare_op=ALU.not_equal, fill=1.0,
                                                base=0, pattern=[[-1, P]], channel_multiplier=1).then_inc(p0_id, 1)
                        for i in range(2):
                            pool.wait_ge(p0_max, (C + 2) * (i + 1))
                            nc.gpsimd.partition_all_reduce(m2[:, i:i + 1], m1[:, i:i + 1], P, RMAX).then_inc(p0_all, 1)

                    @block.vector
                    def _(dve):
                        n = 0
                        for i, (w, b) in enumerate(((stg, bias[:, 0:2 * C]), (stgv, bias[:, 2 * C:3 * C]))):
                            if i == 0:
                                dve.wait_ge(b_in, 16)
                            dve.tensor_reduce(mx[:, i, C:C + 1], b, AX.X, ALU.max, apply_absolute_value=True).then_inc(p0_max, 1)
                            for c in range(C):
                                if i == 0:
                                    dve.wait_ge(in_c[c], 16)
                                elif c == 0:
                                    dve.wait_ge(v_in, 16 * C)
                                dve.tensor_reduce(mx[:, i, c:c + 1], w[:, c, :], AX.X, ALU.max, apply_absolute_value=True).then_inc(p0_max, 1)
                            dve.wait_ge(p0_max, (C + 2) * i + C + 1)
                            dve.tensor_reduce(m1[:, i:i + 1], mx[:, i, :], AX.X, ALU.max).then_inc(p0_max, 1)
                            dve.wait_ge(p0_all, i + 1)
                            n = scale_from_absmax(dve, m2[:, i:i + 1], es[:, i:i + 1], sc[:, i:i + 1], p0_sc, n)
                            if i == 0:
                                dve.tensor_scalar(bqk[:], b, sc[:, 0:1], None, ALU.mult)
                            wd = wqk if i == 0 else wv
                            for c in range(C):
                                dve.wait_ge(p0_hi, C * i + c + 1)
                                dve.scalar_tensor_tensor(out=wd[:, 1, c, :], in0=w[:, c, :], scalar=sc[:, i:i + 1],
                                                         in1=wd[:, 0, c, :], op0=ALU.mult, op1=ALU.subtract)
                        dve.tensor_copy(e_v[:], es[:, 1:2])
                        dve.tensor_copy(s_v[:], sc[:, 1:2])
                        dve.scalar_tensor_tensor(out=exp_scale[:], in0=es[:, 0:1], scalar=float(HD) ** -0.5,
                                                 in1=es[:, 0:1], op0=ALU.mult, op1=ALU.mult)

                    @block.scalar
                    def _(act):
                        for i, (w, wd) in enumerate(((stg, wqk), (stgv, wv))):
                            act.wait_ge(p0_sc, 3 * (i + 1))
                            for c in range(C):
                                nc.scalar.activation(wd[:, 0, c, :], w[:, c, :], ACT.Copy, scale=sc[:, i:i + 1]).then_inc(p0_hi, 1)

            end_phase()

            with ExitStack() as p1:
                xt = sb(p1, "xt", [P, T, H])
                xnT = sb(p1, "xnT", [P, 2, C, S], F16)
                qk_hl = sb(p1, "qk_hl", [P, 2, 2, 2, S], F16)
                qs = sb(p1, "qs", [P, RING, S], F16)
                ks = sb(p1, "ks", [P, RING, S], F16)
                v_sb = sb(p1, "v_sb", [P, T, HEADS_A, V1], F16)
                vg = sb(p1, "vg", [P, 2, T, GH * V1], F16)
                e32 = sb(p1, "e32", [P, 2, 2, S])
                ehi = sb(p1, "ehi", [P, 2, T, S], F16)
                elo = sb(p1, "elo", [P, 2, T, S], F16)
                nmax = sb(p1, "nmax", [P, 2, T])
                nrow = sb(p1, "nrow", [P, 2, T, 2], F16)
                ident16 = sb(p1, "ident16", [P, P], F16)
                sums = sb(p1, "sums", [P, 2, T, V1])
                rsum = sb(p1, "rsum", [P, 2, T])
                csum = sb(p1, "csum", [P, 2, T, HD])
                ctx = sb(p1, "ctx", [P, 2, T, P])
                st6 = sb(p1, "st6", [P, 2, 2, 6])
                mv = sb(p1, "mv", [P, 2, 2])
                rstd = sb(p1, "rstd", [P, 2])
                mhalf = sb(p1, "mhalf", [P, 1])

                st_ps = ps(p1, "st_ps", [P, 2, 2, S])
                ring_ps = ps(p1, "ring_ps", [P, 2, S])
                ctx_ps = ps(p1, "ctx_ps", [P, 512])
                proj_ps = ps(p1, "proj_ps", [P, 512])
                ctx_v = ctx_ps[:, 0:T * V1].rearrange("p (t v) -> p t v", t=T)

                x_in = [sem(f"x_in{t}") for t in range(T)]
                stack_in = [sem(f"stack_in{r}") for r in range(RING)]
                vg_in = [sem(f"vg_in{i}") for i in range(2)]
                ctx_out = [sem(f"ctx_out{i}") for i in range(2)]
                (ring_full, ring_free, st_full, e32_done, ehi_done, elo_dve, elo_pool, pv_done, sums_done, csum_done,
                 rsum_done, ctx_done, max_done, row_hi, row_done, row_in, proj_full, proj_free, hi_done,
                 stat_done, aggr_done, var_done, rstd_done, xn_done, const_done, pool_const) = (sem(n) for n in (
                    "ring_full", "ring_free", "st_full", "e32_done", "ehi_done", "elo_dve", "elo_pool", "pv_done",
                    "sums_done", "csum_done", "rsum_done", "ctx_done", "max_done", "row_hi", "row_done", "row_in",
                    "proj_full", "proj_free", "hi_done", "stat_done", "aggr_done",
                    "var_done", "rstd_done", "xn_done", "const_done", "pool_const"))

                def use_max(h, c):
                    return 5 * h + (c + 1 if c > 1 else c)

                def use_row(h):
                    return 5 * h + 7

                def over(r):
                    return r + 1 if isinstance(r, int) and r < 2 else r

                def unit_T(b, i):
                    return 32 * b + i

                def unit_QK(b, g, qk):
                    return 32 * b + (8 if isinstance(g, int) and g < 2 else 16) + 2 * g + qk

                def unit_V(b, i):
                    return 32 * b + 12 + i

                def live(h):
                    return not isinstance(h, int) or 0 <= h < TOT

                def spread(table, unit, k, quarters):
                    n = 24 // (len(quarters) - 1)
                    for i, q in enumerate(quarters[:-1]):
                        table.setdefault((k + q // 4, q % 4), []).append(unit + (n * i, n * (i + 1)))
                    q = quarters[-1]
                    table.setdefault((k + q // 4, q % 4), []).append(("E",) + unit)

                def fills(gp, last_row):
                    t = {}
                    slow = [1, 2, 3, 4, 5, 6, 7]
                    if gp != 3:
                        spread(t, ("QK", 0, 3, 0), 3, slow)
                        spread(t, ("QK", 0, 3, 1), 5, slow)
                    if gp is None:
                        spread(t, ("QK", 0, 4, 0), 7, slow)
                        spread(t, ("QK", 0, 4, 1), 9, slow)
                    elif gp == 2 and not last_row:
                        for i in range(T):
                            t.setdefault((3 + i, 0), []).append(("LN", i))
                        for i in range(2 * T):
                            t.setdefault((7, i // 2), []).extend([("T", i), ("E", "T", i)])
                        for k, (g, qk) in ((8, (-4, 0)), (9, (-4, 1)), (10, (-3, 0))):
                            spread(t, ("QK", 1, g, qk), k, [0, 1, 2, 3])
                    elif gp == 3 and not last_row:
                        units = [("QK", 1, -5, 1)] + [("V", i) for i in range(2 * T)] + \
                                [("QK", 1, -4, 0), ("QK", 1, -4, 1)]
                        for i, u in enumerate(units):
                            q = 8 * (i // 3) + (0, 3, 6)[i % 3] - (i == 8)
                            spread(t, u, 3, [q, q + 1, q + 2])
                    return t

                def whole_phase(eng, prologue, pair):
                    prologue()
                    pair(0, 0, range(0, 3))
                    if B > 1:
                        with eng.Fori(0, B - 1) as b:
                            with eng.Fori(0, 2) as gp:
                                pair(b, gp, range(3, 11))
                            pair(b, 2, range(3, 11))
                            pair(b, 3, range(3, 11))
                    with eng.Fori(0, 2) as gp:
                        pair(B - 1, gp, range(3, 11))
                    pair(B - 1, 2, range(3, 11), True)
                    pair(B - 1, 3, range(3, 11), True)

                with nc.Block() as block:
                    @block.sync
                    def _(sp):
                        def load_x(b, t):
                            wait(sp, proj_full, unit_T(b, 2 * t + 2) - 32)
                            sp.dma_start(xt[:, t, :], x_t[b, t]).then_inc(x_in[t], 16)

                        def stacks(b, gp, o):
                            m = 8 * b + 2 * gp + o
                            if isinstance(m, int) and not m * GH < TOT:
                                return
                            bb, g = (b + 1, 2 * gp + o - G) if isinstance(gp, int) and 2 * gp + o >= G else (b, 2 * gp + o)
                            sp.wait_ge(proj_free, unit_QK(bb, g, 1) + 1)
                            for i in range(GH):
                                r = (o % 2) * GH + i
                                wait(sp, st_full, 2 * (GH * m + i - RING + 1))
                                for tile, qk, parts in ((qs, 0, (0, 1, 0)), (ks, 1, (0, 0, 1))):
                                    for j, part in enumerate(parts):
                                        sp.dma_start(tile[HD * j:HD * j + HD, r, :],
                                                     qk_hl[HD * i:HD * i + HD, o % 2, qk, part, :]).then_inc(stack_in[r], 16)

                        def values(b, gp, o):
                            m = 8 * b + 2 * gp + o
                            if isinstance(m, int) and not m * GH < TOT:
                                return
                            bb, g = (b + 1, 2 * gp + o - G) if isinstance(gp, int) and 2 * gp + o >= G else (b, 2 * gp + o)
                            wait_apart(sp, proj_free, unit_V(bb, 2 * T))
                            wait(sp, pv_done, 2 * GH * (m - 1))
                            sp.dma_start(vg[:, o % 2].rearrange("p t (h v) -> p t h v", h=GH),
                                         v_sb[:, :, bass.ds(GH * g, GH), :]).then_inc(vg_in[o % 2], 16)

                        def context(b, gp, o):
                            m = 8 * b + 2 * gp + o
                            sp.wait_ge(ctx_done, GH * (m + 1))
                            sp.dma_start(ctx_d[m].rearrange("t p d -> p t d"), ctx[:, o]).then_inc(ctx_out[o], 16)

                        def prologue():
                            for t in range(T):
                                load_x(0, t)
                            for o in range(2):
                                stacks(0, 0, o)
                                values(0, 0, o)

                        def pair(b, gp, slots, last_row=False):
                            for k in slots:
                                if k == 3 and isinstance(gp, int) and gp == 2 and not last_row:
                                    for t in range(T):
                                        load_x(b + 1, t)
                                if k == 4:
                                    stacks(b, gp, 2)
                                if k == 5 and not (isinstance(gp, int) and gp == 3):
                                    values(b, gp, 2)
                                if k == 7:
                                    context(b, gp, 0)
                                if k == 8:
                                    if isinstance(gp, int) and gp == 3:
                                        values(b, gp, 2)
                                    stacks(b, gp, 3)
                                if k == 9:
                                    values(b, gp, 3)
                                if k == 10:
                                    context(b, gp, 1)

                        whole_phase(sp, prologue, pair)
                        for i in range(2):
                            sp.wait_ge(ctx_out[i], 16 * B * G // 2)

                    @block.tensor
                    def _(pe):
                        def max_scores(p, k, c):
                            h = 8 * p + k
                            if not live(h):
                                return
                            r = k % RING
                            if c == 0:
                                pe.wait_ge(stack_in[r], 96 * (p + k // RING + 1))
                            wait(pe, ring_free, over(use_max(h, c) - 2) if live(h - 1) or c else 0)
                            pe.matmul(ring_ps[:, use_max(k, c) % 2, :], qs[0:3 * HD, r, P * c:P * c + P],
                                      ks[0:3 * HD, r, :], start=True, stop=True).then_inc(ring_full, 1)

                        def max_rows(p, k):
                            h = 8 * p + k
                            if not live(h):
                                return
                            pe.wait_ge(row_done, h + 1)
                            wait(pe, ring_free, min(use_row(h) - 2, 5 * TOT - 1) if isinstance(h, int) else use_row(h) - 2)
                            rows = ring_ps[:, use_row(k) % 2, :].bitcast(F16)
                            for c in range(T):
                                mm = pe.transpose(rows[0:2, P * c:P * c + P], nrow[:, k % 2, c, :], ident16[:])
                            mm.then_inc(ring_full, 1)

                        def scores(p, k, c):
                            h, r = 8 * p + k, k % RING
                            if not live(h):
                                return
                            if c == 0:
                                pe.wait_ge(row_in, h + 1)
                            if c % 2 == 0:
                                wait(pe, ehi_done, 2 * h - 1 + c // 2 if live(h - 1) else 0)
                            mm = pe.matmul(st_ps[:, c // 2, c % 2, :], ks[0:3 * HD + 2, r, P * c:P * c + P],
                                           qs[0:3 * HD + 2, r, :], start=True, stop=True)
                            if c % 2:
                                mm.then_inc(st_full, 1)

                        def weighted(p, k, c):
                            h, par, i = 8 * p + k, (k // GH) % 2, k % GH
                            if not live(h):
                                return
                            if c == 0:
                                wait(pe, sums_done, h)
                                if i == 0:
                                    pe.wait_ge(vg_in[par], 16 * (p + k // RING + 1))
                            if c % 2 == 0:
                                pe.wait_ge(ehi_done, 2 * h + 1 + c // 2)
                                pe.wait_ge(elo_pool if c else elo_dve, h + 1)
                            for t in range(T):
                                pe.matmul(ctx_v[:, t, :], ehi[:, k % 2, c, P * t:P * t + P],
                                          vg[:, par, c, V1 * i:V1 * i + V1], start=(c == 0 and t == 0), stop=False,
                                          skip_group_check=True)
                                mm = pe.matmul(ctx_v[:, t, 0:HD + 1], elo[:, k % 2, c, P * t:P * t + P],
                                               vg[:, par, c, V1 * i:V1 * i + HD + 1], start=False,
                                               stop=(c == T - 1), skip_group_check=True)
                            if c % 2:
                                mm.then_inc(pv_done, 1)

                        def qk_part(bb, g, qk, a, z):
                            if a == 0:
                                wait(pe, proj_free, unit_QK(bb, g, qk))
                            for n in range(a, z):
                                c, (wp, xp) = n // 3, ((0, 0), (0, 1), (1, 0))[n % 3]
                                mm = pe.matmul(proj_ps[:], wqk[:, wp, c, bass.ds(H * qk + P * g, P)], xnT[:, xp, c, :],
                                               start=(n == 0), stop=(n == 23))
                            if z == 24:
                                mm.then_inc(proj_full, 1)

                        def v_part(bb, i, a, z):
                            if a == 0:
                                wait(pe, proj_free, unit_V(bb, i))
                            t, half = i // 2, i % 2
                            for n in range(a, z):
                                c, (xp, wp) = n // 3, ((0, 0), (0, 1), (1, 0))[n % 3]
                                mm = pe.matmul(proj_ps[:], xnT[:, xp, c, P * t:P * t + P],
                                               wv[:, wp, c, S * half:S * half + S], start=(n == 0), stop=(n == 23))
                            if z == 24:
                                mm.then_inc(proj_full, 1)

                        def turn(bb, i):
                            wait(pe, proj_free, unit_T(bb, i))
                            if i % 2 == 0:
                                pe.wait_ge(xn_done, T * bb + i // 2 + 1)
                            for c in range(4):
                                h0 = P * (4 * (i % 2) + c)
                                mm = pe.transpose(proj_ps[:, P * c:P * c + P], xt[:, i // 2, h0:h0 + P], ident[:])
                            mm.then_inc(proj_full, 1)

                        def prologue():
                            pe.wait_ge(const_done, 4)
                            for i in range(2 * T):
                                turn(0, i)
                            for g in range(2):
                                for qk in range(2):
                                    qk_part(0, g, qk, 0, 24)
                            for i in range(2 * T):
                                v_part(0, i, 0, 24)
                            for qk in range(2):
                                qk_part(0, 2, qk, 0, 24)
                            for c in range(T):
                                max_scores(0, 0, c)
                            for c in range(T):
                                max_scores(0, 1, c)
                                if c == 1:
                                    max_rows(0, 0)

                        def pair(b, gp, slots, last_row=False):
                            work = fills(gp if isinstance(gp, int) else None, last_row)
                            p = 4 * b + gp
                            for k in slots:
                                for c in range(T):
                                    max_scores(p, k + 2, c)
                                    if c == 1:
                                        max_rows(p, k + 1)
                                    scores(p, k, c)
                                    for f in work.get((k, c), []):
                                        if f[0] == "T":
                                            turn(b + 1, f[1])
                                        elif f[0] == "V":
                                            v_part(b + 1, *f[1:])
                                        elif f[0] == "QK":
                                            qk_part(b + f[1], 2 * gp + f[2], *f[3:])
                                    weighted(p, k - 2, c)

                        whole_phase(pe, prologue, pair)

                    @block.scalar
                    def _(act):
                        def exps(p, k, half):
                            h = 8 * p + k
                            if not live(h):
                                return
                            act.wait_ge(st_full, 2 * h + half + 1)
                            wait(act, elo_pool if half else elo_dve, h)
                            nc.scalar.activation(e32[:, half], st_ps[:, half], ACT.Exp, scale=exp_scale[:, 0:1]).then_inc(e32_done, 1)
                            wait(act, pv_done, 2 * (h - 2) + half + 1)
                            nc.scalar.activation(ehi[:, k % 2, 2 * half:2 * half + 2, :], st_ps[:, half], ACT.Exp,
                                                 scale=exp_scale[:, 0:1]).then_inc(ehi_done, 1)

                        def hi_T(bb, i):
                            act.wait_ge(proj_full, unit_T(bb, i) + 1)
                            t, c0 = i // 2, 4 * (i % 2)
                            nc.scalar.activation(xnT[:, 0, c0:c0 + 4, P * t:P * t + P],
                                                 proj_ps[:].rearrange("p (c n) -> p c n", c=4), ACT.Copy).then_inc(hi_done, 1)

                        def hi_QK(bb, gp, o, qk):
                            g = 2 * gp + o
                            act.wait_ge(proj_full, unit_QK(bb, g, qk) + 1)
                            for i in range(GH):
                                wait(act, stack_in[(o % 2) * GH + i], 96 * (4 * bb + gp + o // 2))
                            nc.scalar.activation(qk_hl[:, o % 2, qk, 0, :], proj_ps[:], ACT.Identity,
                                                 bias=bqk[:, bass.ds(8 * qk + g, 1)]).then_inc(hi_done, 1)

                        def hi_V(bb, i):
                            act.wait_ge(proj_full, unit_V(bb, i) + 1)
                            if i == 0:
                                wait(act, vg_in[0], 64 * bb)
                                wait(act, vg_in[1], 64 * bb)
                            nc.scalar.activation(v_sb[:, i // 2, 16 * (i % 2):16 * (i % 2) + 16, 0:HD],
                                                 proj_ps[:].rearrange("p (h d) -> p h d", d=HD), ACT.Copy).then_inc(hi_done, 1)

                        def prologue():
                            for i in range(2 * T):
                                hi_T(0, i)
                            for g in range(2):
                                for qk in range(2):
                                    hi_QK(0, 0, g, qk)
                            for i in range(2 * T):
                                hi_V(0, i)
                            for qk in range(2):
                                hi_QK(0, 0, 2, qk)

                        def pair(b, gp, slots, last_row=False):
                            work = fills(gp if isinstance(gp, int) else None, last_row)
                            p = 4 * b + gp
                            for k in slots:
                                for c in range(T):
                                    for f in work.get((k, c), []):
                                        if f[0] == "E":
                                            if f[1] == "T":
                                                hi_T(b + 1, f[2])
                                            elif f[1] == "QK":
                                                hi_QK(b + f[2], gp, f[3], f[4])
                                            else:
                                                hi_V(b + 1, f[2])
                                    if c % 2:
                                        exps(p, k, c // 2)

                        whole_phase(act, prologue, pair)

                    @block.vector
                    def _(dve):
                        def max_of(p, k, c):
                            h = 8 * p + k
                            if not live(h):
                                return
                            dve.wait_ge(ring_full, over(use_max(h, c)))
                            dve.tensor_reduce(nmax[:, k % 2, c:c + 1], ring_ps[:, use_max(k, c) % 2, :], AX.X, ALU.max,
                                              negate=True).then_inc(ring_free, 1)

                        def row_parts(p, k):
                            h = 8 * p + k
                            if not live(h):
                                return
                            dve.wait_ge(ring_free, use_max(h, T - 1))
                            dve.tensor_scalar(nrow[:, k % 2, :, 0], nmax[:, k % 2, :], 1.0 / ONES_ROW, None,
                                              ALU.mult).then_inc(row_hi, 1)
                            dve.wait_ge(row_hi, h + 1)
                            dve.scalar_tensor_tensor(out=nrow[:, k % 2, :, 1], in0=nmax[:, k % 2, :], scalar=1.0 / ONES_ROW,
                                                     in1=nrow[:, k % 2, :, 0], op0=ALU.mult, op1=ALU.subtract).then_inc(row_done, 1)

                        def row_stack(p, k):
                            h = 8 * p + k
                            if not live(h):
                                return
                            dve.wait_ge(ring_full, min(use_row(h), 5 * TOT) if isinstance(h, int) else use_row(h))
                            rows = ring_ps[:, use_row(k) % 2, :].bitcast(F16)
                            dve.tensor_copy(qs[3 * HD:3 * HD + 2, k % RING, :], rows[0:2, 0:S]).then_inc(row_in, 1)
                            dve.wait_ge(row_in, h + 1)
                            dve.sem_inc(ring_free, 1)

                        def lo_exps(p, k):
                            h = 8 * p + k
                            if not live(h):
                                return
                            dve.wait_ge(ehi_done, 2 * h + 1)
                            dve.tensor_tensor(elo[:, k % 2, 0:2, :], e32[:, 0], ehi[:, k % 2, 0:2, :],
                                              ALU.subtract).then_inc(elo_dve, 1)

                        def leave_ctx(p, k):
                            h = 8 * p + k
                            if not live(h):
                                return
                            dve.wait_ge(pv_done, 2 * h + 2)
                            dve.reciprocal(rsum[:, k % 2], ctx_v[:, :, HD]).then_inc(rsum_done, 1)
                            dve.tensor_copy(sums[:, k % 2], ctx_v[:]).then_inc(sums_done, 1)

                        def lo_T(bb, i):
                            dve.wait_ge(hi_done, unit_T(bb, i) + 1)
                            t, c0 = i // 2, 4 * (i % 2)
                            dve.tensor_tensor(xnT[:, 1, c0:c0 + 4, P * t:P * t + P], proj_ps[:].rearrange("p (c n) -> p c n", c=4),
                                              xnT[:, 0, c0:c0 + 4, P * t:P * t + P], ALU.subtract).then_inc(proj_free, 1)

                        def lo_QK(bb, gp, o, qk):
                            g = 2 * gp + o
                            dve.wait_ge(hi_done, unit_QK(bb, g, qk) + 1)
                            dve.scalar_tensor_tensor(out=qk_hl[:, o % 2, qk, 1, :], in0=proj_ps[:],
                                                     scalar=bqk[:, bass.ds(8 * qk + g, 1)], in1=qk_hl[:, o % 2, qk, 0, :],
                                                     op0=ALU.add, op1=ALU.subtract).then_inc(proj_free, 1)

                        def lo_V(bb, i):
                            dve.wait_ge(hi_done, unit_V(bb, i) + 1)
                            hs = slice(16 * (i % 2), 16 * (i % 2) + 16)
                            dve.tensor_tensor(v_sb[:, i // 2, hs, HD + 1:V1], proj_ps[:].rearrange("p (h d) -> p h d", d=HD),
                                              v_sb[:, i // 2, hs, 0:HD], ALU.subtract).then_inc(proj_free, 1)

                        def stats(bb, t):
                            dve.wait_ge(x_in[t], 16 * (bb + 1))
                            wait(dve, xn_done, T * bb + t - 1)
                            for i in range(2):
                                dve.bn_stats(st6[:, t % 2, i, :], xt[:, t, S * i:S * i + S]).then_inc(stat_done, 1)
                            wait_apart(dve, stat_done, 2 * (T * bb + t + 1))
                            dve.bn_aggr(mv[:, t % 2], st6[:, t % 2].rearrange("p a b -> p (a b)")).then_inc(aggr_done, 1)

                        def prologue():
                            dve.memset(mhalf[:], -0.5).then_inc(const_done, 1)
                            dve.memset(v_sb[:, :, :, HD:HD + 1], 1.0).then_inc(const_done, 1)
                            dve.memset(ks[3 * HD:3 * HD + 2], ONES_ROW).then_inc(const_done, 1)
                            dve.tensor_copy(ident16[:], ident[:]).then_inc(const_done, 1)
                            for t in range(T):
                                stats(0, t)
                            for i in range(2 * T):
                                lo_T(0, i)
                            for g in range(2):
                                for qk in range(2):
                                    lo_QK(0, 0, g, qk)
                            for i in range(2 * T):
                                lo_V(0, i)
                            for qk in range(2):
                                lo_QK(0, 0, 2, qk)
                            for c in range(T):
                                max_of(0, 0, c)
                            row_parts(0, 0)
                            for c in range(T):
                                max_of(0, 1, c)
                                if c == 1:
                                    row_stack(0, 0)
                            row_parts(0, 1)

                        def pair(b, gp, slots, last_row=False):
                            work = fills(gp if isinstance(gp, int) else None, last_row)
                            p = 4 * b + gp
                            for k in slots:
                                for c in range(T):
                                    if c == 0:
                                        leave_ctx(p, k - 3)
                                    max_of(p, k + 2, c)
                                    if c == 1:
                                        row_stack(p, k + 1)
                                    if c == T - 1:
                                        row_parts(p, k + 2)
                                    if c == 0:
                                        lo_exps(p, k - 1)
                                    for f in work.get((k, c), []):
                                        if f[0] == "LN":
                                            stats(b + 1, f[1])
                                        elif f[0] == "E":
                                            if f[1] == "T":
                                                lo_T(b + 1, f[2])
                                            elif f[1] == "QK":
                                                lo_QK(b + f[2], gp, f[3], f[4])
                                            else:
                                                lo_V(b + 1, f[2])

                        whole_phase(dve, prologue, pair)

                    @block.gpsimd
                    def _(pool):
                        def lo_exps(p, k):
                            h = 8 * p + k
                            if not live(h):
                                return
                            pool.wait_ge(ehi_done, 2 * h + 2)
                            nc.gpsimd.tensor_tensor(elo[:, k % 2, 2:4, :], e32[:, 1], ehi[:, k % 2, 2:4, :],
                                                    ALU.subtract).then_inc(elo_pool, 1)

                        def normalise(p, k):
                            h, par, i = 8 * p + k, (k // GH) % 2, k % GH
                            if not live(h):
                                return
                            pool.wait_ge(sums_done, h + 1)
                            nc.gpsimd.tensor_tensor(csum[:, k % 2], sums[:, k % 2, :, 0:HD], sums[:, k % 2, :, HD + 1:V1],
                                                    ALU.add).then_inc(csum_done, 1)
                            if i == 0:
                                wait(pool, ctx_out[par], 16 * (p + k // RING))
                            pool.wait_ge(rsum_done, h + 1)
                            pool.wait_ge(csum_done, h + 1)
                            nc.gpsimd.tensor_tensor(ctx[:, par, :, HD * i:HD * i + HD], csum[:, k % 2],
                                                    rsum[:, k % 2].unsqueeze(2).to_broadcast([P, T, HD]),
                                                    ALU.mult).then_inc(ctx_done, 1)

                        def layer_norm(bb, t):
                            n = T * bb + t
                            wait_apart(pool, aggr_done, n + 1)
                            nc.gpsimd.tensor_scalar(rstd[:, t % 2:t % 2 + 1], mv[:, t % 2, 1:2], LN_EPS, None, ALU.add).then_inc(var_done, 1)
                            pool.wait_ge(var_done, n + 1)
                            nc.gpsimd.tensor_tensor(rstd[:, t % 2:t % 2 + 1], rstd[:, t % 2:t % 2 + 1], mhalf[:], ALU.pow).then_inc(rstd_done, 1)
                            wait_apart(pool, rstd_done, n + 1)
                            nc.gpsimd.tensor_scalar(xt[:, t, :], xt[:, t, :], mv[:, t % 2, 0:1], rstd[:, t % 2:t % 2 + 1],
                                                    ALU.subtract, ALU.mult).then_inc(xn_done, 1)

                        def prologue():
                            for t in range(T):
                                layer_norm(0, t)

                        def pair(b, gp, slots, last_row=False):
                            work = fills(gp if isinstance(gp, int) else None, last_row)
                            p = 4 * b + gp
                            for k in slots:
                                for c in range(T):
                                    for f in work.get((k, c), []):
                                        if f[0] == "LN":
                                            layer_norm(b + 1, f[1])
                                    if c == 0:
                                        normalise(p, k - 3)
                                    if c == 1:
                                        lo_exps(p, k - 1)

                        whole_phase(pool, prologue, pair)

        end_phase()

        with ExitStack() as p234:
            hit_rows = sb(p234, "hit_rows", [NC, H], F16)
            centT = sb(p234, "centT", [P, 2, C, NC], F16)
            fbias = sb(p234, "fbias", [P, H])
            hits = sb(p234, "hits", [P, 2, NC])
            ones = sb(p234, "ones", [P, P])
            qsel = sb(p234, "qsel", [P, 2, B * T])
            e_w = sb(p234, "e_w", [P, 3])
            cent_scale = sb(p234, "cent_scale", [P, 1])
            mhalf = sb(p234, "mhalf2", [P, 1])

            with ExitStack() as p2:
                stg = sb(p2, "stg2", [P, C, H])
                wo = sb(p2, "wo", [P, 2, C, H], F16)
                wT = sb(p2, "wT", [P, 2, C, H], F16)
                cst = sb(p2, "cst", [NC, H])
                asg = sb(p2, "asg", [NC, H], I32)
                asgf = sb(p2, "asgf", [NC, H])
                cid = sb(p2, "cid", [NC, 1], I32)
                cidf = sb(p2, "cidf", [NC, 1])
                mx, m1, m2, sc = (sb(p2, n, [P, 3]) for n in ("mx2", "m12", "m22", "sc2"))
                bv = sb(p2, "bv", [P, H])
                obias = sb(p2, "obias", [P, H])
                inv_o = sb(p2, "inv_o", [P, 1])
                ct = sb(p2, "ct", [P, T, H])
                xb = sb(p2, "xb", [P, T, H])
                cT = sb(p2, "cT", [P, 2, 2, C, P], F16)
                hit = HitTiles(sb, p2, "2")
                cT_ps = ps(p2, "cT_ps", [P, 2, 512])
                o_ps = ps(p2, "o_ps", [P, 2, 512])
                x_ps = ps(p2, "x_ps", [P, 2, 512])
                c_ps = ps(p2, "c_ps", [P, 512])
                (row_in2, ow_in, fw_in, ct_in2, max2, all2, sc2, wo_hi, wo_lo, w_turned, w_hi, w_lo, c_turned, c_hi,
                 c_lo, misc2, inv2, cx_done, xb_done, cT_full, cT_hi, cT_lo, o_full, x1_done, id2, cid_done) = (
                    sem(n) for n in ("row_in2", "ow_in", "fw_in", "ct_in2", "max2", "all2", "sc2", "wo_hi", "wo_lo",
                                     "w_turned", "w_hi", "w_lo", "c_turned", "c_hi", "c_lo", "misc2", "inv2",
                                     "cx_done", "xb_done", "cT_full", "cT_hi", "cT_lo", "o_full", "x1_done",
                                     "id2", "cid_done"))
                wT_out = sem("wT_out")
                tile_in = [sem(f"tile_in{t}") for t in range(T)]
                store2 = [sem(f"store2_{t}") for t in range(T)]
                hs = HitSems(sem, "2")

                def steps(eng, step, first=3):
                    for n in range(-1, first):
                        step(0, n)
                    if B > 1:
                        with eng.Fori(0, B - 1) as b:
                            for k in range(first, first + T):
                                step(b, k)
                    for k in range(first, first + T):
                        step(B - 1, k)

                def tile(b, k):
                    n = T * b + k
                    return not isinstance(n, int) or 0 <= n < T * B, n

                with nc.Block() as block:
                    @block.sync
                    def _(sp):
                        sp.dma_start(stg[:], ow.rearrange("(c p) n -> p c n", p=P)).then_inc(ow_in, 16)
                        sp.dma_start(cst[:], cent).then_inc(ct_in2, 16)
                        sp.dma_start(bv[:], qkvb[2 * H:3 * H].partition_broadcast(P)).then_inc(row_in2, 16)
                        sp.dma_start(obias[:], ob.partition_broadcast(P)).then_inc(row_in2, 16)
                        sp.dma_start(fbias[:], fb.partition_broadcast(P)).then_inc(row_in2, 16)
                        sp.dma_start(asg[:], assign.partition_broadcast(NC)).then_inc(row_in2, 16)
                        sp.wait_ge(wo_lo, C)
                        sp.dma_start(stg[:], fw.rearrange("(o p) i -> p o i", p=P)).then_inc(fw_in, 16)

                        def load(b, k):
                            ok, n = tile(b, k)
                            if not ok:
                                return
                            t = k % T
                            wait(sp, store2[t], 32 * (b + k // T))
                            bb = b + k // T
                            sp.dma_start(ct[:, t].rearrange("p (g d) -> p g d", d=P),
                                         ctx_t[bb, :, t].rearrange("g p d -> p g d")).then_inc(tile_in[t], 16)
                            sp.dma_start(xb[:, t], x_t[bb, t]).then_inc(tile_in[t], 16)

                        def store(b, k):
                            ok, n = tile(b, k)
                            if not ok:
                                return
                            sp.wait_ge(x1_done, 2 * n + 2)
                            sp.dma_start(x1_d[n], ct[:, k % T]).then_inc(store2[k % T], 16)
                            sp.wait_ge(hs.lo, 2 * n + 2)
                            sp.dma_start(xT1_d[n], hit.xT[:, k % 2]).then_inc(store2[k % T], 16)

                        def step(b, k):
                            store(b, k - 2)
                            load(b, k + 2)

                        load(0, 0)
                        sp.wait_ge(w_lo, 2 * C)
                        sp.dma_start(wT_d, wT[:]).then_inc(wT_out, 16)
                        steps(sp, step, 2)
                        sp.wait_ge(wT_out, 16)
                        for t in range(T):
                            sp.wait_ge(store2[t], 32 * B)

                    @block.tensor
                    def _(pe):
                        pe.wait_ge(ct_in2, 16)
                        for c in range(C):
                            mm = pe.transpose(c_ps[:, NC * c:NC * c + NC], cst[:, P * c:P * c + P], ident[0:NC, 0:NC])
                        mm.then_inc(c_turned, 1)
                        pe.wait_ge(fw_in, 16)
                        for i in range(2 * C):
                            c, half = i // 2, i % 2
                            wait(pe, w_lo, i - 1)
                            for o in range(4):
                                mm = pe.transpose(cT_ps[:, i % 2, P * o:P * o + P], stg[:, 4 * half + o, P * c:P * c + P], ident[:])
                            mm.then_inc(w_turned, 1)

                        def turn_context(b, k):
                            ok, n = tile(b, k)
                            if not ok:
                                return
                            pe.wait_ge(cx_done, n + 1)
                            if isinstance(n, int) and n == 0:
                                pe.wait_ge(w_lo, 2 * C)
                            for half in range(2):
                                wait(pe, cT_lo, 2 * n - 1 + half if not isinstance(n, int) or n > 0 else 0)
                                for c in range(4):
                                    h0 = P * (4 * half + c)
                                    mm = pe.transpose(cT_ps[:, half, P * c:P * c + P], ct[:, k % T, h0:h0 + P], ident[:])
                                mm.then_inc(cT_full, 1)

                        def project(b, k):
                            ok, n = tile(b, k)
                            if not ok:
                                return
                            pe.wait_ge(cT_lo, 2 * n + 2)
                            if isinstance(n, int) and n == 0:
                                pe.wait_ge(wo_lo, C)
                            for half in range(2):
                                wait(pe, x1_done, 2 * n - 1 + half if not isinstance(n, int) or n > 0 else 0)
                                for i in range(24):
                                    c, (xp, wp) = i // 3, ((0, 0), (0, 1), (1, 0))[i % 3]
                                    mm = pe.matmul(o_ps[:, half, :], cT[:, k % 2, xp, c, :], wo[:, wp, c, 512 * half:512 * half + 512],
                                                   start=(i == 0), stop=(i == 23))
                                mm.then_inc(o_full, 1)

                        def step(b, k):
                            turn_context(b, k + 1)
                            if tile(b, k - 2)[0]:
                                hit_turn(pe, hs, hit, x_ps, xb[:, (k - 2) % T], ident, tile(b, k - 2)[1], k % 2)
                            project(b, k)
                            if tile(b, k - 2)[0]:
                                hit_logits(pe, hs, hit, c_ps, centT, tile(b, k - 2)[1], k % 2)

                        pe.wait_ge(c_lo, 1)
                        steps(pe, step)

                    @block.scalar
                    def _(act):
                        act.wait_ge(sc2, 3)
                        for c in range(C):
                            nc.scalar.activation(wo[:, 0, c, :], stg[:, c, :], ACT.Copy, scale=sc[:, 0:1]).then_inc(wo_hi, 1)
                        act.wait_ge(sc2, 6)
                        act.wait_ge(c_turned, 1)
                        nc.scalar.activation(centT[:, 0], c_ps[:, 0:C * NC].rearrange("p (c n) -> p c n", c=C), ACT.Copy,
                                             scale=sc[:, 1:2]).then_inc(c_hi, 1)
                        act.wait_ge(sc2, 9)
                        for i in range(2 * C):
                            act.wait_ge(w_turned, i + 1)
                            nc.scalar.activation(wT[:, 0, i // 2, 512 * (i % 2):512 * (i % 2) + 512], cT_ps[:, i % 2, :], ACT.Copy,
                                                 scale=sc[:, 2:3]).then_inc(w_hi, 1)

                        def hi_context(b, k):
                            ok, n = tile(b, k)
                            if not ok:
                                return
                            wait(act, o_full, 2 * n - 2)
                            for half in range(2):
                                act.wait_ge(cT_full, 2 * n + half + 1)
                                nc.scalar.activation(cT[:, k % 2, 0, 4 * half:4 * half + 4, :],
                                                     cT_ps[:, half, :].rearrange("p (c n) -> p c n", c=4), ACT.Copy).then_inc(cT_hi, 1)

                        def step(b, k):
                            hi_context(b, k + 1)
                            if tile(b, k - 2)[0]:
                                hit_hi(act, nc, hs, hit, x_ps, tile(b, k - 2)[1], k % 2, store2, k - 2, b)
                                hit_exp(act, nc, hs, hit, c_ps, cent_scale, tile(b, k - 2)[1], k % 2)

                        steps(act, step)

                    @block.vector
                    def _(dve):
                        dve.memset(m1[:], 0.0).then_inc(misc2, 1)
                        dve.memset(mhalf[:], -0.5).then_inc(misc2, 1)
                        dve.memset(hits[:], 0.0).then_inc(misc2, 1)
                        dve.memset(ones[:], 1.0).then_inc(misc2, 1)
                        dve.wait_ge(misc2, 4)
                        dve.wait_ge(ow_in, 16)
                        dve.tensor_reduce(m1[:, 0:1], stg[:], AX.XY, ALU.max, apply_absolute_value=True).then_inc(max2, 1)
                        dve.wait_ge(all2, 1)
                        n = scale_from_absmax(dve, m2[:, 0:1], e_w[:, 0:1], sc[:, 0:1], sc2, 0)
                        for c in range(C):
                            dve.wait_ge(wo_hi, c + 1)
                            dve.scalar_tensor_tensor(out=wo[:, 1, c, :], in0=stg[:, c, :], scalar=sc[:, 0:1], in1=wo[:, 0, c, :],
                                                     op0=ALU.mult, op1=ALU.subtract).then_inc(wo_lo, 1)
                        dve.tensor_tensor(inv_o[:], e_w[:, 0:1], e_v[:], ALU.mult).then_inc(inv2, 1)
                        dve.wait_ge(ct_in2, 16)
                        dve.tensor_reduce(m1[0:NC, 1:2], cst[:], AX.X, ALU.max, apply_absolute_value=True).then_inc(max2, 1)
                        dve.wait_ge(all2, 2)
                        n = scale_from_absmax(dve, m2[:, 1:2], e_w[:, 1:2], sc[:, 1:2], sc2, n)
                        dve.tensor_scalar(cent_scale[:], e_w[:, 1:2], 1.0 / TEMPERATURE, None, ALU.mult).then_inc(inv2, 1)
                        dve.wait_ge(c_hi, 1)
                        dve.scalar_tensor_tensor(out=centT[:, 1], in0=c_ps[:, 0:C * NC].rearrange("p (c n) -> p c n", c=C),
                                                 scalar=sc[:, 1:2], in1=centT[:, 0], op0=ALU.mult, op1=ALU.subtract).then_inc(c_lo, 1)
                        dve.wait_ge(row_in2, 64)
                        dve.tensor_scalar(bv[:], bv[:], s_v[:, 0:1], None, ALU.mult).then_inc(inv2, 1)
                        dve.wait_ge(cid_done, 1)
                        dve.tensor_copy(asgf[:], asg[:]).then_inc(misc2, 1)
                        dve.tensor_copy(cidf[:], cid[:]).then_inc(misc2, 1)
                        dve.wait_ge(misc2, 6)
                        dve.tensor_scalar(hit_rows[:], asgf[:], cidf[:, 0:1], None, ALU.is_equal)
                        dve.wait_ge(fw_in, 16)
                        dve.tensor_reduce(m1[:, 2:3], stg[:], AX.XY, ALU.max, apply_absolute_value=True).then_inc(max2, 1)
                        dve.wait_ge(all2, 3)
                        scale_from_absmax(dve, m2[:, 2:3], e_w[:, 2:3], sc[:, 2:3], sc2, n)
                        for i in range(2 * C):
                            cols = slice(512 * (i % 2), 512 * (i % 2) + 512)
                            dve.wait_ge(w_hi, i + 1)
                            dve.scalar_tensor_tensor(out=wT[:, 1, i // 2, cols], in0=cT_ps[:, i % 2, :], scalar=sc[:, 2:3],
                                                     in1=wT[:, 0, i // 2, cols], op0=ALU.mult, op1=ALU.subtract).then_inc(w_lo, 1)

                        def lo_context(b, k):
                            ok, n = tile(b, k)
                            if not ok:
                                return
                            for half in range(2):
                                dve.wait_ge(cT_hi, 2 * n + half + 1)
                                dve.tensor_tensor(cT[:, k % 2, 1, 4 * half:4 * half + 4, :],
                                                  cT_ps[:, half, :].rearrange("p (c n) -> p c n", c=4),
                                                  cT[:, k % 2, 0, 4 * half:4 * half + 4, :], ALU.subtract).then_inc(cT_lo, 1)

                        def residual(b, k):
                            ok, n = tile(b, k)
                            if not ok:
                                return
                            dve.wait_ge(xb_done, n + 1)
                            if isinstance(n, int) and n == 0:
                                dve.wait_ge(inv2, 3)
                            for half in range(2):
                                cols = slice(512 * half, 512 * half + 512)
                                dve.wait_ge(o_full, 2 * n + half + 1)
                                dve.scalar_tensor_tensor(out=ct[:, k % T, cols], in0=o_ps[:, half, :], scalar=inv_o[:, 0:1],
                                                         in1=xb[:, k % T, cols], op0=ALU.mult, op1=ALU.add).then_inc(x1_done, 1)
                            dve.wait_ge(x1_done, 2 * n + 2)
                            hit_stats(dve, hs, hit, ct[:, k % T], n, k % 2)

                        def step(b, k):
                            lo_context(b, k + 1)
                            if tile(b, k - 2)[0]:
                                hit_lo(dve, hs, hit, x_ps, tile(b, k - 2)[1], k % 2)
                            residual(b, k)
                            if tile(b, k - 2)[0]:
                                hit_select(dve, hs, hit, c_ps, cent_scale, hits[:, 0], qsel[:, 0], tile(b, k - 2)[1], k % 2)

                        steps(dve, step)

                    @block.gpsimd
                    def _(pool):
                        nc.gpsimd.iota(cid[:], pattern=[[0, 1]], base=0, channel_multiplier=1).then_inc(cid_done, 1)
                        for i in range(3):
                            pool.wait_ge(max2, i + 1)
                            nc.gpsimd.partition_all_reduce(m2[:, i:i + 1], m1[:, i:i + 1], P, RMAX).then_inc(all2, 1)
                        pool.wait_ge(inv2, 3)

                        def biases(b, k):
                            ok, n = tile(b, k)
                            if not ok:
                                return
                            pool.wait_ge(tile_in[k % T], 32 * (b + k // T + 1))
                            nc.gpsimd.tensor_tensor(ct[:, k % T], ct[:, k % T], bv[:], ALU.add).then_inc(cx_done, 1)
                            nc.gpsimd.tensor_tensor(xb[:, k % T], xb[:, k % T], obias[:], ALU.add).then_inc(xb_done, 1)

                        def step(b, k):
                            biases(b, k + 1)
                            ok, n = tile(b, k - 1)
                            if ok:
                                hit_norm(pool, nc, hs, hit, ct[:, (k - 1) % T], xb[:, (k - 1) % T], mhalf, n, (k - 1) % 2)

                        steps(pool, step)

            end_phase()

            D = H // HEADS_B
            with ExitStack() as p3:
                wm = sb(p3, "wm", [P, 2, C, H], F16)
                hrow = sb(p3, "hrow", [P, H])
                vb = sb(p3, "vb", [P, H])
                csel = sb(p3, "csel", [NC, P], F16)
                mask = sb(p3, "mask", [P, H], F16)
                alpha = sb(p3, "alpha", [P, HEADS_B])
                cq = sb(p3, "cq", [P, C])
                m3, e3, s3 = (sb(p3, n, [P, 2]) for n in ("m3", "e3", "s3"))
                sig_scale = sb(p3, "sig_scale", [P, 1])
                inv_f = sb(p3, "inv_f", [P, B * T])
                x2 = sb(p3, "x2", [P, 2, T, H])
                xn2 = sb(p3, "xn2", [P, T, H])
                xn3 = sb(p3, "xn3", [P, T, H])
                fxT = sb(p3, "fxT", [P, 2, 2, C, P], F16)
                xhT = sb(p3, "xhT", [P, 2, C, S], F16)
                yT = sb(p3, "yT", [P, 2, C, S], F16)
                vv = sb(p3, "vv", [P, 2, T, H], F16)
                a32 = sb(p3, "a32", [P, T, S])
                ahl = sb(p3, "ahl", [P, 2, T, S], F16)
                h3T = sb(p3, "h3T", [P, 2, 2, C, P], F16)
                ln2, ln3 = LnTiles(sb, p3, "_x2"), LnTiles(sb, p3, "_x3")
                c4 = sb(p3, "c4", [P, T, NC])
                cm, cs = sb(p3, "cm3", [P, T]), sb(p3, "cs3", [P, T])
                h4 = sb(p3, "h4", [P, 2, T, NC])
                t_ps = ps(p3, "t_ps", [P, 512])
                l_ps = ps(p3, "l_ps", [P, 512])
                f_ps = ps(p3, "f_ps", [P, 2, 512])
                s_ps = ps(p3, "s_ps", [P, 2, 512])
                pv_ps = ps(p3, "pv_ps", [P, 2, 2, D])

                names = ("bind_in", "p3c", "p3all", "p3sc", "csum3", "csel3", "mask_full", "mask3", "wm_done", "cT3", 
                         "xb3", "f_full", "x2_done", "n_full", "n_hi",
                         "n_lo", "v32", "v_hi", "v_lo", "s_full", "sig", "tri", "a_hi", "a_lo", "pv_full", "x3_done",
                         "h_full", "h_hi", "h_lo", "l_full", "lmax", "lsub", "lexp", "lsum", "lthr", "lhit", "lacc")
                q = {n: sem(n + "_3" if not n.endswith("3") else n) for n in names}
                w_in3 = sem("w_in3")
                ls2, ls3 = LnSems(sem, "_x2"), LnSems(sem, "_x3")
                x1_in = [sem(f"x1_in{t}") for t in range(T)]
                fxT_in = [sem(f"fxT_in{t}") for t in range(2)]
                x3_out = [sem(f"x3_out{t}") for t in range(T)]
                h3_out = [sem(f"h3_out{t}") for t in range(2)]

                def row(b):
                    return not isinstance(b, int) or 0 <= b < B

                def batch_rows(eng, step):
                    step(-1, 1)
                    step(0, 0)
                    if B > 2:
                        with eng.Fori(0, (B - 2) // 2) as r:
                            step(2 * r + 1, 1)
                            step(2 * r + 2, 0)
                    for b in range(max(1, 2 * ((B - 2) // 2) + 1), B + 1):
                        step(b, b % 2)

                with nc.Block() as block:
                    @block.sync
                    def _(sp):
                        sp.dma_start(wm[:], wT_d).then_inc(w_in3, 16)
                        sp.dma_start(fbias[:], fb.partition_broadcast(P)).then_inc(q["bind_in"], 16)
                        for dst, src in ((hrow, bvq), (xn2[:, 0], bvk), (vb, bvv)):
                            sp.dma_start(dst[:], src.rearrange("h d -> (h d)").partition_broadcast(P)).then_inc(q["bind_in"], 16)

                        def loads(b, par, t):
                            if not row(b):
                                return
                            wait(sp, q["f_full"], 8 * b + 2 * t - 2)
                            sp.dma_start(fxT[:, t % 2], xT1_d[T * b + t]).then_inc(fxT_in[t % 2], 16)
                            wait_apart(sp, ls3.xn, T * (b - 2) + t + 1 if not isinstance(b, int) or b > 1 else 0)
                            wait(sp, x3_out[t], 16 * (b - 1))
                            sp.dma_start(x2[:, par, t], x1_d[T * b + t]).then_inc(x1_in[t], 16)

                        def step(b, par):
                            if row(b - 1):
                                for t in range(T):
                                    sp.wait_ge(q["x3_done"], 8 * b)
                                    sp.dma_start(x3_d[T * (b - 1) + t], x2[:, 1 - par, t]).then_inc(x3_out[t], 16)
                            for t in range(T):
                                loads(b + 1, 1 - par, t)
                                if row(b - 1) and t >= 2:
                                    store_h(b - 1, t - 2)
                            if row(b - 1):
                                store_h(b - 1, 2)
                                store_h(b - 1, 3)

                        def store_h(b, t):
                            sp.wait_ge(q["h_lo"], 8 * b + 2 * t + 2)
                            sp.dma_start(xT3_d[T * b + t], h3T[:, t % 2]).then_inc(h3_out[t % 2], 16)

                        for t in range(2):
                            sp.sem_inc(h3_out[t], 16)
                        batch_rows(sp, step)
                        for t in range(T):
                            sp.wait_ge(x3_out[t], 16 * B)
                        for t in range(2):
                            sp.wait_ge(h3_out[t], 32 * B + 16)

                    @block.tensor
                    def _(pe):
                        pe.matmul(l_ps[0:NC, 0:P], hits[:, 0], ones[:], start=True, stop=True).then_inc(q["csum3"], 1)
                        pe.wait_ge(q["csel3"], 1)
                        for half in range(2):
                            pe.matmul(f_ps[:, half, :], csel[:], hit_rows[:, 512 * half:512 * half + 512], start=True,
                                      stop=True).then_inc(q["mask_full"], 1)
                        pe.wait_ge(q["p3sc"], 1)
                        for half in range(2):
                            wait(pe, q["cT3"], half)
                            for c in range(4):
                                h0 = P * (4 * half + c)
                                mm = pe.transpose(t_ps[:, P * c:P * c + P], hrow[:, h0:h0 + P], ident[:])
                            mm.then_inc(q["p3c"], 1)
                        pe.wait_ge(q["wm_done"], 2)

                        def turn2(b, i):
                            if not row(b):
                                return
                            if i % 2 == 0:
                                pe.wait_ge(ls2.xn, T * b + i // 2 + 1)
                            wait(pe, q["n_lo"], 8 * b + i)
                            for c in range(4):
                                h0 = P * (4 * (i % 2) + c)
                                mm = pe.transpose(t_ps[:, P * c:P * c + P], xn2[:, i // 2, h0:h0 + P], ident[:])
                            mm.then_inc(q["n_full"], 1)

                        def ffn(b, u, a, z):
                            if not row(b):
                                return
                            t, half = u // 2, u % 2
                            if a == 0:
                                if half == 0:
                                    pe.wait_ge(fxT_in[t % 2], 32 * b + 16 * (t // 2) + 16)
                                wait(pe, q["x2_done"], 8 * b + u - 1)
                            for n in range(a, z):
                                c, (xp, wp) = n // 3, ((0, 0), (0, 1), (1, 0))[n % 3]
                                mm = pe.matmul(f_ps[:, half, :], fxT[:, t % 2, xp, c, :], wm[:, wp, c, 512 * half:512 * half + 512],
                                               start=(n == 0), stop=(n == 23))
                            if z == 24:
                                mm.then_inc(q["f_full"], 1)

                        def scores_b(b, hd):
                            if not row(b):
                                return
                            if hd == 0:
                                pe.wait_ge(q["n_lo"], 8 * b + 8)
                            for c in range(T):
                                wait(pe, q["sig"], 16 * b + 4 * hd + c - 1)
                                for i in range(6):
                                    d, (xp, yp) = 2 * hd + i // 3, ((0, 0), (0, 1), (1, 0))[i % 3]
                                    mm = pe.matmul(s_ps[:, c % 2, P * c:S], xhT[:, xp, d, P * c:P * c + P], yT[:, yp, d, P * c:S],
                                                   start=(i == 0), stop=(i == 5))
                                mm.then_inc(q["s_full"], 1)

                        def turn3(b, t, half):
                            if not row(b):
                                return
                            if half == 0:
                                pe.wait_ge(ls3.xn, T * b + t + 1)
                            if t == 0 and half == 0:
                                pe.wait_ge(q["n_lo"], 8 * min(b + 2, B) if isinstance(b, int) else 8 * (b + 2))
                            else:
                                pe.wait_ge(q["h_lo"], 8 * b + 2 * t + half)
                            for c in range(4):
                                h0 = P * (4 * half + c)
                                mm = pe.transpose(t_ps[:, P * c:P * c + P], xn3[:, t, h0:h0 + P], ident[:])
                            mm.then_inc(q["h_full"], 1)

                        def weighted_b(b, hd):
                            if not row(b):
                                return
                            pe.wait_ge(q["a_lo"], 16 * b + 4 * hd + 4)
                            if hd == 0:
                                pe.wait_ge(q["v_lo"], T * (b + 1))
                            for t in range(T):
                                if t % 2 == 0:
                                    wait(pe, q["x3_done"], 8 * b + 2 * hd - 1 + t // 2 if not isinstance(b, int) or b > 0 or hd > 0 else 0)
                                last = 3 * (t + 1) - 1
                                for n in range(last + 1):
                                    c, (ap_, vp) = n // 3, ((0, 0), (0, 1), (1, 0))[n % 3]
                                    mm = pe.matmul(pv_ps[:, t // 2, t % 2, :], ahl[:, ap_, c, P * t:P * t + P],
                                                   vv[:, vp, c, D * hd:D * hd + D], start=(n == 0), stop=(n == last))
                                if t % 2:
                                    mm.then_inc(q["pv_full"], 1)

                        def logits(b, t):
                            if not row(b):
                                return
                            pe.wait_ge(q["h_lo"], 8 * b + 2 * t + 2)
                            if t == 0 and isinstance(b, int):
                                wait(pe, q["lsub"], b)
                            for n in range(24):
                                c, (xp, wp) = n // 3, ((0, 0), (0, 1), (1, 0))[n % 3]
                                mm = pe.matmul(l_ps[:, NC * t:NC * t + NC], h3T[:, t % 2, xp, c, :], centT[:, wp, c, :],
                                               start=(n == 0), stop=(n == 23))
                            mm.then_inc(q["l_full"], 1)

                        def step(b, par):
                            for i in range(2 * T):
                                turn2(b, i)
                                ffn(b + 1, i // 2, 12 * (i % 2), 12 * (i % 2) + 12)
                            for hd in range(HEADS_B):
                                scores_b(b, hd)
                                turn3(b - 1, hd, 0)
                                ffn(b + 1, 4 + hd, 0, 24)
                                turn3(b - 1, hd, 1)
                                weighted_b(b, hd)
                                logits(b - 1, hd)

                        batch_rows(pe, step)

                    @block.scalar
                    def _(act):
                        def hi2(b, i):
                            if not row(b):
                                return
                            act.wait_ge(q["n_full"], 8 * b + i + 1)
                            if i == 0:
                                wait(act, q["s_full"], 16 * b)
                            t, c0 = i // 2, 4 * (i % 2)
                            nc.scalar.activation(xhT[:, 0, c0:c0 + 4, P * t:P * t + P], t_ps[:].rearrange("p (c n) -> p c n", c=4),
                                                 ACT.Copy).then_inc(q["n_hi"], 1)
                            for c in range(4):
                                nc.scalar.activation(yT[:, 0, c0 + c, P * t:P * t + P], t_ps[:, P * c:P * c + P], ACT.Copy,
                                                     scale=cq[:, c0 + c:c0 + c + 1]).then_inc(q["n_hi"], 1)

                        def hi_v(b, t):
                            if not row(b):
                                return
                            act.wait_ge(q["v32"], T * b + t + 1)
                            if t == 0:
                                wait(act, q["pv_full"], 8 * b)
                            nc.scalar.activation(vv[:, 0, t], hrow[:], ACT.Copy).then_inc(q["v_hi"], 1)

                        def sigmoids(b, hd):
                            if not row(b):
                                return
                            wait(act, q["a_lo"], 16 * b + 4 * hd)
                            for c in range(T):
                                act.wait_ge(q["s_full"], 16 * b + 4 * hd + c + 1)
                                nc.scalar.activation(a32[:, c, P * c:S], s_ps[:, c % 2, P * c:S], ACT.Sigmoid,
                                                     scale=sig_scale[:, 0:1]).then_inc(q["sig"], 1)

                        def hi_a(b, hd):
                            if not row(b):
                                return
                            wait(act, q["pv_full"], 8 * b + 2 * hd)
                            for c in range(T):
                                act.wait_ge(q["tri"], 16 * b + 4 * hd + c + 1)
                                nc.scalar.activation(ahl[:, 0, c, P * c:S], a32[:, c, P * c:S], ACT.Copy).then_inc(q["a_hi"], 1)

                        def hi3(b, t, half):
                            if not row(b):
                                return
                            act.wait_ge(q["h_full"], 8 * b + 2 * t + half + 1)
                            if half == 0:
                                act.wait_ge(h3_out[t % 2], 32 * b + 16 * (t // 2) + 16)
                            nc.scalar.activation(h3T[:, t % 2, 0, 4 * half:4 * half + 4, :], t_ps[:].rearrange("p (c n) -> p c n", c=4),
                                                 ACT.Copy).then_inc(q["h_hi"], 1)

                        def step(b, par):
                            for i in range(2 * T):
                                hi2(b, i)
                                if i % 2:
                                    hi_v(b, i // 2)
                            for hd in range(HEADS_B):
                                sigmoids(b, hd)
                                hi3(b - 1, hd, 0)
                                hi_a(b, hd)
                                hi3(b - 1, hd, 1)
                            if row(b - 1):
                                act.wait_ge(q["lsub"], b)
                                nc.scalar.activation(c4[:], c4[:], ACT.Exp, scale=cent_scale[:, 0:1]).then_inc(q["lexp"], 1)

                        act.wait_ge(q["cT3"], 2)
                        batch_rows(act, step)

                    @block.vector
                    def _(dve):
                        k = [0]

                        def chain(ins):
                            k[0] += 1
                            ins.then_inc(q["mask3"], 1)
                            dve.wait_ge(q["mask3"], k[0])

                        dve.wait_ge(q["csum3"], 1)
                        dve.tensor_scalar(csel[:], l_ps[0:NC, 0:P], 0.5, None, ALU.is_gt).then_inc(q["csel3"], 1)
                        dve.wait_ge(q["bind_in"], 64)
                        tmp = xn3[:, 0]
                        for w in (hrow[:], xn2[:, 0], vb[:]):
                            wh = w.rearrange("p (h d) -> p h d", h=HEADS_B)
                            chain(dve.tensor_reduce(alpha[:], wh, AX.X, ALU.add, apply_absolute_value=True))
                            chain(dve.tensor_scalar(alpha[:], alpha[:], 1.0 / D, None, ALU.mult))
                            chain(dve.tensor_scalar(tmp, w, 0.0, 2.0, ALU.is_ge, ALU.mult))
                            chain(dve.tensor_scalar(tmp, tmp, -1.0, None, ALU.add))
                            chain(dve.tensor_tensor(tmp.rearrange("p (h d) -> p h d", h=HEADS_B), tmp.rearrange("p (h d) -> p h d", h=HEADS_B),
                                                    alpha[:].unsqueeze(2).to_broadcast([P, HEADS_B, D]), ALU.mult))
                            chain(dve.tensor_tensor(tmp, tmp, w, ALU.subtract))
                            chain(dve.tensor_tensor(w, tmp, w, ALU.add))
                        chain(dve.tensor_tensor(hrow[:], hrow[:], xn2[:, 0], ALU.mult))
                        chain(dve.tensor_reduce(m3[:, 0:1], hrow[:], AX.X, ALU.max, apply_absolute_value=True))
                        chain(dve.tensor_reduce(m3[:, 1:2], vb[:], AX.X, ALU.max, apply_absolute_value=True))
                        scale_from_absmax(dve, m3[:], e3[:], s3[:], q["p3all"], 0)
                        chain(dve.tensor_scalar(sig_scale[:], e3[:, 0:1], 4.0 * float(D) ** -0.5, None, ALU.mult))
                        chain(dve.tensor_scalar(vb[:], vb[:], s3[:, 1:2], None, ALU.mult))
                        chain(dve.tensor_scalar(hrow[:], hrow[:], s3[:, 0:1], None, ALU.mult))
                        chain(dve.tensor_scalar(inv_f[:], qsel[:, 0], e_w[:, 2:3], None, ALU.mult))
                        chain(dve.memset(h4[:], 0.0))
                        dve.sem_inc(q["p3sc"], 1)
                        for half in range(2):
                            dve.wait_ge(q["mask_full"], half + 1)
                            chain(dve.tensor_copy(mask[:, 512 * half:512 * half + 512], f_ps[:, half, :]))
                        chain(dve.tensor_tensor(fbias[:], fbias[:], mask[:], ALU.mult))
                        dve.wait_ge(w_in3, 16)
                        for part in range(2):
                            dve.tensor_tensor(wm[:, part], wm[:, part], mask[:].unsqueeze(1).to_broadcast([P, C, H]),
                                              ALU.mult).then_inc(q["wm_done"], 1)
                        for half in range(2):
                            dve.wait_ge(q["p3c"], half + 1)
                            dve.tensor_copy(cq[:, 4 * half:4 * half + 4].unsqueeze(2), t_ps[:].rearrange("p (c n) -> p c n", c=4)[:, :, 0:1]).then_inc(q["cT3"], 1)
                        dve.wait_ge(q["cT3"], 2)

                        def bias_x1(b, par, t):
                            if not row(b):
                                return
                            dve.wait_ge(x1_in[t], 16 * (b + 1))
                            dve.scalar_tensor_tensor(out=x2[:, par, t], in0=fbias[:], scalar=qsel[:, 0, bass.ds(T * b + t, 1)],
                                                     in1=x2[:, par, t], op0=ALU.mult, op1=ALU.add).then_inc(q["xb3"], 1)
                            dve.wait_ge(q["xb3"], T * b + t + 1)

                        def residual(b, par, u):
                            if not row(b):
                                return
                            t, half = u // 2, u % 2
                            if half == 0:
                                bias_x1(b, par, t)
                            cols = slice(512 * half, 512 * half + 512)
                            dve.wait_ge(q["f_full"], 8 * b + u + 1)
                            dve.scalar_tensor_tensor(out=x2[:, par, t, cols], in0=f_ps[:, half, :], scalar=inv_f[:, bass.ds(T * b + t, 1)],
                                                     in1=x2[:, par, t, cols], op0=ALU.mult, op1=ALU.add).then_inc(q["x2_done"], 1)
                            if half:
                                dve.wait_ge(q["x2_done"], 8 * b + u + 1)

                        def lo2(b, i):
                            if not row(b):
                                return
                            t, c0 = i // 2, 4 * (i % 2)
                            dve.wait_ge(q["n_hi"], 5 * (8 * b + i + 1))
                            dve.tensor_tensor(xhT[:, 1, c0:c0 + 4, P * t:P * t + P], t_ps[:].rearrange("p (c n) -> p c n", c=4),
                                              xhT[:, 0, c0:c0 + 4, P * t:P * t + P], ALU.subtract)
                            for c in range(4):
                                mm = dve.scalar_tensor_tensor(out=yT[:, 1, c0 + c, P * t:P * t + P], in0=t_ps[:, P * c:P * c + P],
                                                              scalar=cq[:, c0 + c:c0 + c + 1], in1=yT[:, 0, c0 + c, P * t:P * t + P],
                                                              op0=ALU.mult, op1=ALU.subtract)
                            mm.then_inc(q["n_lo"], 1)

                        def lo_v(b, t):
                            if not row(b):
                                return
                            dve.wait_ge(q["v_hi"], T * b + t + 1)
                            dve.tensor_tensor(vv[:, 1, t], hrow[:], vv[:, 0, t], ALU.subtract).then_inc(q["v_lo"], 1)

                        def lo3(b, t, half):
                            if not row(b):
                                return
                            dve.wait_ge(q["h_hi"], 8 * b + 2 * t + half + 1)
                            dve.tensor_tensor(h3T[:, t % 2, 1, 4 * half:4 * half + 4, :], t_ps[:].rearrange("p (c n) -> p c n", c=4),
                                              h3T[:, t % 2, 0, 4 * half:4 * half + 4, :], ALU.subtract).then_inc(q["h_lo"], 1)

                        def lo_a(b, hd):
                            if not row(b):
                                return
                            for c in range(T):
                                dve.wait_ge(q["a_hi"], 16 * b + 4 * hd + c + 1)
                                dve.tensor_tensor(ahl[:, 1, c, P * c:S], a32[:, c, P * c:S], ahl[:, 0, c, P * c:S],
                                                  ALU.subtract).then_inc(q["a_lo"], 1)

                        def add_b(b, par, hd):
                            if not row(b):
                                return
                            for i in range(2):
                                dve.wait_ge(q["pv_full"], 8 * b + 2 * hd + i + 1)
                                xs = x2[:, par, 2 * i:2 * i + 2, D * hd:D * hd + D]
                                dve.scalar_tensor_tensor(out=xs, in0=pv_ps[:, i], scalar=e3[:, 1:2], in1=xs,
                                                         op0=ALU.mult, op1=ALU.add).then_inc(q["x3_done"], 1)

                        def select(b):
                            if not row(b):
                                return
                            lg = l_ps[:, 0:T * NC].rearrange("p (t c) -> p t c", t=T)
                            dve.wait_ge(q["l_full"], T * b + T)
                            dve.tensor_reduce(cm[:], lg, AX.X, ALU.max).then_inc(q["lmax"], 1)
                            dve.wait_ge(q["lmax"], b + 1)
                            dve.tensor_tensor(c4[:], lg, cm[:].unsqueeze(2).to_broadcast([P, T, NC]), ALU.subtract).then_inc(q["lsub"], 1)
                            dve.wait_ge(q["lexp"], b + 1)
                            dve.tensor_reduce(cs[:], c4[:], AX.X, ALU.add).then_inc(q["lsum"], 1)
                            dve.wait_ge(q["lsum"], b + 1)
                            dve.tensor_scalar(cs[:], cs[:], HIT, None, ALU.mult).then_inc(q["lthr"], 1)
                            dve.wait_ge(q["lthr"], b + 1)
                            dve.tensor_tensor(h4[:, 0], c4[:], cs[:].unsqueeze(2).to_broadcast([P, T, NC]), ALU.is_gt).then_inc(q["lhit"], 1)
                            dve.wait_ge(q["lhit"], b + 1)
                            dve.tensor_reduce(qsel[:, 1, bass.ds(T * b, T)], h4[:, 0], AX.X, ALU.max)
                            dve.tensor_tensor(h4[:, 1], h4[:, 1], h4[:, 0], ALU.max).then_inc(q["lacc"], 1)

                        def step(b, par):
                            for i in range(2 * T):
                                if i % 2 == 0:
                                    ln3_stats(b, par, i // 2)
                                lo2(b, i)
                                if i % 2:
                                    lo_v(b, i // 2)
                                    residual(b + 1, 1 - par, i // 2)
                                    if i % 4 == 3:
                                        ln2_stats(b, par, i // 4)
                            for hd in range(HEADS_B):
                                lo3(b - 1, hd, 0)
                                lo_a(b, hd)
                                residual(b + 1, 1 - par, 4 + hd)
                                if hd % 2:
                                    ln2_stats(b, par, 2 + hd // 2)
                                lo3(b - 1, hd, 1)
                                add_b(b, par, hd)
                            select(b - 1)

                        def ln3_stats(b, par, t):
                            if row(b - 1):
                                dve.wait_ge(q["x3_done"], 8 * b)
                                if t >= 2:
                                    dve.wait_ge(ls3.xn, T * (b - 1) + t - 1)
                                hit_stats(dve, ls3, ln3, x2[:, 1 - par, t], T * (b - 1) + t, t % 2)

                        def ln2_stats(b, par, t):
                            if row(b + 1):
                                wait(dve, ls2.xn, T * (b + 1) + t - 1)
                                hit_stats(dve, ls2, ln2, x2[:, 1 - par, t], T * (b + 1) + t, t % 2)

                        batch_rows(dve, step)
                        dve.wait_ge(q["lacc"], B)
                        chain(dve.tensor_tensor(h4[:, 1, 0:2], h4[:, 1, 0:2], h4[:, 1, 2:4], ALU.max))
                        dve.tensor_tensor(hits[:, 1], h4[:, 1, 0], h4[:, 1, 1], ALU.max)

                    @block.gpsimd
                    def _(pool):
                        def norm3(b, par, t):
                            if not row(b - 1):
                                return
                            if isinstance(b, int):
                                wait(pool, q["h_full"], 8 * (b - 2) + 2 * t + 2 if b > 1 else 0)
                            hit_norm(pool, nc, ls3, ln3, x2[:, 1 - par, t], xn3[:, t], mhalf, T * (b - 1) + t, t % 2)

                        def norm2(b, par, t):
                            if not row(b + 1):
                                return
                            wait(pool, q["n_full"], 8 * b + 2 * t + 2 if not isinstance(b, int) or b >= 0 else 0)
                            hit_norm(pool, nc, ls2, ln2, x2[:, 1 - par, t], xn2[:, t], mhalf, T * (b + 1) + t, t % 2)

                        def values(b, t):
                            if not row(b):
                                return
                            pool.wait_ge(ls2.xn, T * b + t + 1)
                            wait(pool, q["v_lo"], T * b + t)
                            nc.gpsimd.tensor_tensor(hrow[:], xn2[:, t], vb[:], ALU.mult).then_inc(q["v32"], 1)

                        def triangle(b, hd):
                            if not row(b):
                                return
                            for c in range(T):
                                wait_apart(pool, q["sig"], 16 * b + 4 * hd + c + 1)
                                diag = a32[:, c, P * c:P * c + P]
                                nc.gpsimd.affine_select(out=diag, in_=diag, compare_op=ALU.is_ge, fill=0.0, base=0,
                                                        pattern=[[1, P]], channel_multiplier=-1).then_inc(q["tri"], 1)

                        def step(b, par):
                            for i in range(2 * T):
                                if i % 2 == 0:
                                    norm3(b, par, i // 2)
                                else:
                                    values(b, i // 2)
                                if i % 4 == 3:
                                    norm2(b, par, i // 4)
                            for hd in range(HEADS_B):
                                triangle(b, hd)
                                if hd % 2:
                                    norm2(b, par, 2 + hd // 2)

                        pool.wait_ge(q["cT3"], 2)
                        batch_rows(pool, step)

            end_phase()

            with ExitStack() as p4:
                wm = sb(p4, "wm4", [P, 2, C, H], F16)
                csel = sb(p4, "csel4", [NC, P], F16)
                mask = sb(p4, "mask4", [P, H], F16)
                inv_f = sb(p4, "inv_f4", [P, B * T])
                xT = sb(p4, "xT4", [P, T, 2, C, P], F16)
                x3 = sb(p4, "x34", [P, T, H])
                l_ps = ps(p4, "l_ps4", [P, 512])
                f_ps = ps(p4, "f_ps4", [P, 2, 2, 512])
                bias_in, csum4, csel4, mask_full, prep4, wm4, f_full, xb4, x4 = (sem(n) for n in (
                    "bias_in4", "csum4", "csel4", "mask_full4", "prep4", "wm_done4", "f_full4", "xb4", "x4_done"))
                w_in4 = sem("w_in4")
                x_in4 = [sem(f"x_in4_{t}") for t in range(T)]
                x_out4 = [sem(f"x_out4_{t}") for t in range(T)]

                def rows4(eng, step):
                    for t in range(T):
                        step(0, t)
                    if B > 1:
                        with eng.Fori(1, B) as b:
                            for t in range(T):
                                step(b, t)

                with nc.Block() as block:
                    @block.sync
                    def _(sp):
                        sp.dma_start(wm[:], wT_d).then_inc(w_in4, 16)
                        sp.dma_start(fbias[:], fb.partition_broadcast(P)).then_inc(bias_in, 16)

                        def step(b, t):
                            wait(sp, x_out4[t], 16 * b)
                            sp.dma_start(xT[:, t], xT3_d[T * b + t]).then_inc(x_in4[t], 16)
                            sp.dma_start(x3[:, t], x3_d[T * b + t]).then_inc(x_in4[t], 16)

                        rows4(sp, step)
                        for t in range(T):
                            sp.wait_ge(x_out4[t], 16 * B)

                    @block.tensor
                    def _(pe):
                        pe.matmul(l_ps[0:NC, 0:P], hits[:, 1], ones[:], start=True, stop=True).then_inc(csum4, 1)
                        pe.wait_ge(csel4, 1)
                        for half in range(2):
                            pe.matmul(f_ps[:, 0, half, :], csel[:], hit_rows[:, 512 * half:512 * half + 512], start=True,
                                      stop=True).then_inc(mask_full, 1)
                        pe.wait_ge(wm4, 2)

                        def step(b, t):
                            pe.wait_ge(x_in4[t], 32 * (b + 1))
                            for half in range(2):
                                wait(pe, x4, 8 * b + 2 * t + half - 3)
                                for n in range(24):
                                    c, (xp, wp) = n // 3, ((0, 0), (0, 1), (1, 0))[n % 3]
                                    mm = pe.matmul(f_ps[:, t % 2, half, :], xT[:, t, xp, c, :], wm[:, wp, c, 512 * half:512 * half + 512],
                                                   start=(n == 0), stop=(n == 23))
                                mm.then_inc(f_full, 1)

                        rows4(pe, step)

                    @block.scalar
                    def _(act):
                        def step(b, t):
                            act.wait_ge(x4, 8 * b + 2 * t + 2)
                            act.dma_start(out_t[T * b + t], x3[:, t]).then_inc(x_out4[t], 16)

                        rows4(act, step)

                    @block.vector
                    def _(dve):
                        dve.wait_ge(csum4, 1)
                        dve.tensor_scalar(csel[:], l_ps[0:NC, 0:P], 0.5, None, ALU.is_gt).then_inc(csel4, 1)
                        dve.tensor_scalar(inv_f[:], qsel[:, 1], e_w[:, 2:3], None, ALU.mult).then_inc(prep4, 1)
                        for half in range(2):
                            dve.wait_ge(mask_full, half + 1)
                            dve.tensor_copy(mask[:, 512 * half:512 * half + 512], f_ps[:, 0, half, :]).then_inc(prep4, 1)
                        dve.wait_ge(prep4, 3)
                        dve.wait_ge(w_in4, 16)
                        for part in range(2):
                            dve.tensor_tensor(wm[:, part], wm[:, part], mask[:].unsqueeze(1).to_broadcast([P, C, H]),
                                              ALU.mult).then_inc(wm4, 1)
                        dve.wait_ge(bias_in, 16)
                        dve.tensor_tensor(fbias[:], fbias[:], mask[:], ALU.mult).then_inc(prep4, 1)
                        dve.wait_ge(prep4, 4)

                        def step(b, t):
                            dve.wait_ge(x_in4[t], 32 * (b + 1))
                            dve.scalar_tensor_tensor(out=x3[:, t], in0=fbias[:], scalar=qsel[:, 1, bass.ds(T * b + t, 1)],
                                                     in1=x3[:, t], op0=ALU.mult, op1=ALU.add).then_inc(xb4, 1)
                            dve.wait_ge(xb4, T * b + t + 1)
                            for half in range(2):
                                cols = slice(512 * half, 512 * half + 512)
                                dve.wait_ge(f_full, 8 * b + 2 * t + half + 1)
                                dve.scalar_tensor_tensor(out=x3[:, t, cols], in0=f_ps[:, t % 2, half, :],
                                                         scalar=inv_f[:, bass.ds(T * b + t, 1)], in1=x3[:, t, cols],
                                                         op0=ALU.mult, op1=ALU.add).then_inc(x4, 1)

                        rows4(dve, step)


_INS = ['L0_attn_a_x', 'L0_attn_a_attn_qkvw', 'L0_attn_a_attn_qkvb', 'L0_attn_a_attn_ow', 'L0_attn_a_attn_ob',
        'L0_attn_b_bv_q', 'L0_attn_b_bv_k', 'L0_attn_b_bv_v', 'L0_ffn_weight', 'L0_ffn_bias', 'L0_ffn_centroids',
        'L0_ffn_assignments']


def kernel(**inputs):
    import numpy as _np
    import concourse.bacc as _bacc
    from concourse import mybir as _mybir
    from concourse.bass_utils import run_bass_kernel_spmd as _run

    nc = _bacc.Bacc("TRN2", target_bir_lowering=False, num_devices=1)
    arrays, args = {}, []
    for name in _INS:
        a = _np.ascontiguousarray(inputs[name])
        arrays[f"in_{name}_dram"] = a
        args.append(nc.dram_tensor(f"in_{name}_dram", a.shape, _mybir.dt.from_np(a.dtype), kind="ExternalInput").ap())
    shape = inputs['L0_attn_a_x'].shape
    args.append(nc.dram_tensor("out_0_dram", shape, _mybir.dt.float32, kind="ExternalOutput").ap())
    hybrid_layer(nc, *args)
    r = _run(nc, [arrays], core_ids=[0])
    return r.results[0]["out_0_dram"]
```

```python
from contextlib import ExitStack

import concourse.bass as bass
from concourse import mybir

P = 128
ALU = mybir.AluOpType
ACT = mybir.ActivationFunctionType
AX = mybir.AxisListType
F32 = mybir.dt.float32
F16 = mybir.dt.float16
I32 = mybir.dt.int32
RMAX = bass.bass_isa.ReduceOp.max

HEADS_A = 32
HEADS_B = 4
LN_EPS = 1e-5
HIT = 0.01
TEMPERATURE = 0.1
EXP_MASK = 0x7F800000
EXP_TWICE = 0x7F000000
ONES_ROW = 16384.0
GH = 4
NC = 64
RING = 8


def wait(eng, sem, value):
    if not (isinstance(value, int) and value <= 0):
        eng.wait_ge(sem, value)


def wait_apart(eng, sem, value):
    if isinstance(value, int):
        wait(eng, sem, value)
    else:
        value = eng.to_reg(value)
        eng.wait_ge(sem, 1)
        eng.wait_ge(sem, value)


def scale_from_absmax(dve, m, e, s, done, n):
    dve.tensor_scalar(m, m, 1e-30, 8e37, ALU.max, ALU.min).then_inc(done, 1)
    dve.wait_ge(done, n + 1)
    dve.tensor_single_scalar(e.bitcast(I32), m.bitcast(I32), EXP_MASK, ALU.bitwise_and).then_inc(done, 1)
    dve.wait_ge(done, n + 2)
    dve.tensor_scalar(s.bitcast(I32), e.bitcast(I32), -1.0, float(EXP_TWICE), ALU.mult, ALU.add).then_inc(done, 1)
    dve.wait_ge(done, n + 3)
    return n + 3


class LnTiles:

    def __init__(self, sb, stack, n):
        self.st6 = sb(stack, "st6" + n, [P, 2, 2, 6])
        self.mv = sb(stack, "mv" + n, [P, 2, 2])
        self.rstd = sb(stack, "rstd" + n, [P, 2])


class HitTiles(LnTiles):

    def __init__(self, sb, stack, n):
        super().__init__(sb, stack, n)
        self.xT = sb(stack, "xT" + n, [P, 2, 2, 8, P], F16)
        self.nm = sb(stack, "nm" + n, [P, 2])
        self.bias = sb(stack, "bias" + n, [P, 2])
        self.e = sb(stack, "e" + n, [P, 2, NC])
        self.sum = sb(stack, "sum" + n, [P, 2])
        self.thr = sb(stack, "thr" + n, [P, 2])
        self.hit = sb(stack, "hit" + n, [P, 2, NC])


class LnSems:

    def __init__(self, sem, n):
        self.stat, self.aggr, self.var, self.rstd, self.xn = (sem(f"{a}{n}") for a in ("stat", "aggr", "var", "rstd", "xn"))


class HitSems(LnSems):

    def __init__(self, sem, n):
        super().__init__(sem, n)
        self.turned, self.hi, self.lo, self.logits, self.nmax, self.bias, self.exp, self.thr, self.hit, self.acc = (
            sem(f"hit_{a}{n}") for a in ("turned", "hi", "lo", "logits", "nmax", "bias", "exp", "thr", "hit", "acc"))


def hit_stats(dve, hs, t, x, n, par):
    for i in range(2):
        dve.bn_stats(t.st6[:, par, i, :], x[:, 512 * i:512 * i + 512]).then_inc(hs.stat, 1)
    wait_apart(dve, hs.stat, 2 * n + 2)
    dve.bn_aggr(t.mv[:, par], t.st6[:, par].rearrange("p a b -> p (a b)")).then_inc(hs.aggr, 1)


def hit_rstd(pool, nc, hs, t, mhalf, n, par):
    wait_apart(pool, hs.aggr, n + 1)
    r = t.rstd[:, par:par + 1]
    nc.gpsimd.tensor_scalar(r, t.mv[:, par, 1:2], LN_EPS, None, ALU.add).then_inc(hs.var, 1)
    pool.wait_ge(hs.var, n + 1)
    nc.gpsimd.tensor_tensor(r, r, mhalf[:], ALU.pow).then_inc(hs.rstd, 1)


def hit_norm(dve, hs, t, x, xn, n, par):
    dve.wait_ge(hs.rstd, n + 1)
    dve.tensor_scalar(xn, x, t.mv[:, par, 0:1], t.rstd[:, par:par + 1], ALU.subtract, ALU.mult).then_inc(hs.xn, 1)


def hit_turn(pe, hs, t, x_ps, xn, ident, n, par):
    pe.wait_ge(hs.xn, n + 1)
    for half in range(2):
        wait(pe, hs.lo, 2 * n - 1 + half if not isinstance(n, int) or n > 0 else 0)
        for c in range(4):
            h0 = P * (4 * half + c)
            mm = pe.transpose(x_ps[:, half, P * c:P * c + P], xn[:, h0:h0 + P], ident[:])
        mm.then_inc(hs.turned, 1)


def hit_hi(act, nc, hs, t, x_ps, n, par, stored, k, b):
    wait(act, hs.logits, n - 1)
    wait(act, stored[(k - 2) % len(stored)], 32 * (b + (k - 2) // len(stored) + 1) if not isinstance(n, int) or n > 1 else 0)
    for half in range(2):
        act.wait_ge(hs.turned, 2 * n + half + 1)
        nc.scalar.activation(t.xT[:, par, 0, 4 * half:4 * half + 4, :],
                             x_ps[:, half, :].rearrange("p (c n) -> p c n", c=4), ACT.Copy).then_inc(hs.hi, 1)


def hit_lo(dve, hs, t, x_ps, n, par):
    for half in range(2):
        dve.wait_ge(hs.hi, 2 * n + half + 1)
        dve.tensor_tensor(t.xT[:, par, 1, 4 * half:4 * half + 4, :], x_ps[:, half, :].rearrange("p (c n) -> p c n", c=4),
                          t.xT[:, par, 0, 4 * half:4 * half + 4, :], ALU.subtract).then_inc(hs.lo, 1)


def hit_logits(pe, hs, t, c_ps, centT, n, par):
    pe.wait_ge(hs.lo, 2 * n + 2)
    wait(pe, hs.exp, n)
    for i in range(24):
        c, (xp, wp) = i // 3, ((0, 0), (0, 1), (1, 0))[i % 3]
        mm = pe.matmul(c_ps[:, 0:NC], t.xT[:, par, xp, c, :], centT[:, wp, c, :], start=(i == 0), stop=(i == 23))
    mm.then_inc(hs.logits, 1)


def hit_exp(act, nc, hs, t, c_ps, cent_scale, n, par):
    act.wait_ge(hs.bias, n + 1)
    nc.scalar.activation(t.e[:, par], c_ps[:, 0:NC], ACT.Exp, bias=t.bias[:, par:par + 1], scale=cent_scale[:, 0:1],
                         accum_out=t.sum[:, par:par + 1]).then_inc(hs.exp, 1)


def hit_select(dve, hs, t, c_ps, cent_scale, hits, qsel, n, par):
    one = slice(par, par + 1)
    dve.wait_ge(hs.logits, n + 1)
    dve.tensor_reduce(t.nm[:, one], c_ps[:, 0:NC], AX.X, ALU.max, negate=True).then_inc(hs.nmax, 1)
    dve.wait_ge(hs.nmax, n + 1)
    dve.tensor_scalar(t.bias[:, one], t.nm[:, one], cent_scale[:, 0:1], None, ALU.mult).then_inc(hs.bias, 1)
    dve.wait_ge(hs.exp, n + 1)
    dve.tensor_scalar(t.thr[:, one], t.sum[:, one], HIT, None, ALU.mult).then_inc(hs.thr, 1)
    dve.wait_ge(hs.thr, n + 1)
    dve.tensor_scalar(t.hit[:, par], t.e[:, par], t.thr[:, one], None, ALU.is_gt).then_inc(hs.hit, 1)
    dve.wait_ge(hs.hit, n + 1)
    dve.tensor_reduce(qsel[:, bass.ds(n, 1)], t.hit[:, par], AX.X, ALU.max)
    dve.tensor_tensor(hits, hits, t.hit[:, par], ALU.max).then_inc(hs.acc, 1)


def hybrid_layer(nc, x, qkvw, qkvb, ow, ob, bvq, bvk, bvv, fw, fb, cent, assign, out):
    B, S, H = x.shape
    C = H // P
    T = S // P
    HD = H // HEADS_A
    G = HEADS_A // GH
    assert HD * GH == P and S == 512 and H == 1024 and G == 8 and T == 4
    TOT = B * HEADS_A
    V1 = 2 * HD + 1

    ctx_d = nc.dram_tensor("ctx_scratch", (B * G, T, P, P), F32).ap()

    x1_d = nc.dram_tensor("x1_scratch", (B * T, P, H), F32).ap()
    x3_d = nc.dram_tensor("x3_scratch", (B * T, P, H), F32).ap()
    wT_d = nc.dram_tensor("wT_scratch", (P, 2, C, H), F16).ap()
    xT1_d = nc.dram_tensor("xT1_scratch", (B * T, P, 2, C, P), F16).ap()
    xT3_d = nc.dram_tensor("xT3_scratch", (B * T, P, 2, C, P), F16).ap()

    x_t = x.rearrange("b (t p) h -> b t p h", p=P)
    out_t = out.rearrange("b (t p) h -> (b t) p h", p=P)
    ctx_t = ctx_d.rearrange("(b g) t p d -> b g t p d", g=G)

    with ExitStack() as top:
        phase_sems = []

        def sem(name):
            phase_sems.append(nc.alloc_semaphore(name=name))
            return phase_sems[-1]

        def end_phase():
            nc.clear_and_free_semaphores(list(phase_sems))
            phase_sems.clear()
            nc.all_engine_barrier()

        def sb(stack, name, shape, dt=F32):
            return stack.enter_context(nc.sbuf_tensor(name, shape, dt))

        def ps(stack, name, shape):
            return stack.enter_context(nc.psum_tensor(name, shape, F32))

        ident = sb(top, "ident", [P, P])
        e_v = sb(top, "e_v", [P, 1])
        s_v = sb(top, "s_v", [P, 1])

        with ExitStack() as p01:
            wqk = sb(p01, "wqk", [P, 2, C, 2 * H], F16)
            wv = sb(p01, "wv", [P, 2, C, H], F16)
            bqk = sb(p01, "bqk", [P, 2 * H // P])
            exp_scale = sb(p01, "exp_scale", [P, 1])

            with ExitStack() as p0:
                stg = sb(p0, "stg", [P, C, 2 * H])
                stgv = sb(p0, "stgv", [P, C, H])
                mx = sb(p0, "mx", [P, 2, C + 1])
                bias = sb(p0, "bias", [P, 3 * H // P])
                m1 = sb(p0, "m1", [P, 2])
                m2 = sb(p0, "m2", [P, 2])
                es = sb(p0, "es", [P, 2])
                sc = sb(p0, "sc", [P, 2])
                v_in, b_in = sem("v_in"), sem("b_in")
                p0_max, p0_all, p0_sc, p0_hi, p0_id, p0_vs = (sem(n) for n in ("p0_max", "p0_all", "p0_sc", "p0_hi", "p0_id", "p0_vs"))
                V_LO_POOL = C // 4
                in_c = [sem(f"wc_in{c}") for c in range(C)]
                with nc.Block() as block:
                    @block.sync
                    def _(sp):
                        w_c = qkvw.rearrange("(c p) n -> c p n", p=P)
                        for c in range(C):
                            sp.dma_start(stg[:, c, :], w_c[c, :, 0:2 * H]).then_inc(in_c[c], 16)
                        for c in range(C):
                            sp.dma_start(stgv[:, c, :], w_c[c, :, 2 * H:3 * H]).then_inc(v_in, 16)

                    @block.gpsimd
                    def _(pool):
                        with nc.allow_non_contiguous_dma(reason="a small bias, one feature per partition"):
                            pool.dma_start(bias[:], qkvb.rearrange("(c p) -> p c", p=P)).then_inc(b_in, 16)
                        nc.gpsimd.memset(ident[:], 0.0).then_inc(p0_id, 1)
                        pool.wait_ge(p0_id, 1)
                        nc.gpsimd.affine_select(out=ident[:], in_=ident[:], compare_op=ALU.not_equal, fill=1.0,
                                                base=0, pattern=[[-1, P]], channel_multiplier=1).then_inc(p0_id, 1)
                        for i in range(2):
                            pool.wait_ge(p0_max, (C + 2) * (i + 1))
                            nc.gpsimd.partition_all_reduce(m2[:, i:i + 1], m1[:, i:i + 1], P, RMAX).then_inc(p0_all, 1)
                        pool.wait_ge(p0_sc, 6)
                        for c in range(V_LO_POOL):
                            pool.wait_ge(p0_hi, C + c + 1)
                            nc.gpsimd.tensor_scalar(stgv[:, c, :], stgv[:, c, :], sc[:, 1:2], None, ALU.mult).then_inc(p0_vs, 1)
                            pool.wait_ge(p0_vs, c + 1)
                            nc.gpsimd.tensor_tensor(wv[:, 1, c, :], stgv[:, c, :], wv[:, 0, c, :], ALU.subtract)

                    @block.vector
                    def _(dve):
                        def lo_qk(c):
                            dve.wait_ge(p0_hi, c + 1)
                            dve.scalar_tensor_tensor(out=wqk[:, 1, c, :], in0=stg[:, c, :], scalar=sc[:, 0:1],
                                                     in1=wqk[:, 0, c, :], op0=ALU.mult, op1=ALU.subtract)

                        for i, (w, b) in enumerate(((stg, bias[:, 0:2 * C]), (stgv, bias[:, 2 * C:3 * C]))):
                            for c in range(C):
                                if i == 0:
                                    dve.wait_ge(in_c[c], 16)
                                elif c == 0:
                                    dve.wait_ge(v_in, 16 * C)
                                dve.tensor_reduce(mx[:, i, c:c + 1], w[:, c, :], AX.X, ALU.max, apply_absolute_value=True).then_inc(p0_max, 1)
                            if i == 0:
                                dve.wait_ge(b_in, 16)
                            dve.tensor_reduce(mx[:, i, C:C + 1], b, AX.X, ALU.max, apply_absolute_value=True).then_inc(p0_max, 1)
                            dve.wait_ge(p0_max, (C + 2) * i + C + 1)
                            dve.tensor_reduce(m1[:, i:i + 1], mx[:, i, :], AX.X, ALU.max).then_inc(p0_max, 1)
                            dve.wait_ge(p0_all, i + 1)
                            scale_from_absmax(dve, m2[:, i:i + 1], es[:, i:i + 1], sc[:, i:i + 1], p0_sc, 3 * i)
                            if i == 0:
                                for c in range(C // 2):
                                    lo_qk(c)
                        dve.tensor_scalar(bqk[:], bias[:, 0:2 * C], sc[:, 0:1], None, ALU.mult)
                        for c in range(C // 2, C):
                            lo_qk(c)
                        for c in range(V_LO_POOL, C):
                            dve.wait_ge(p0_hi, C + c + 1)
                            dve.scalar_tensor_tensor(out=wv[:, 1, c, :], in0=stgv[:, c, :], scalar=sc[:, 1:2],
                                                     in1=wv[:, 0, c, :], op0=ALU.mult, op1=ALU.subtract)
                        dve.tensor_copy(e_v[:], es[:, 1:2])
                        dve.tensor_copy(s_v[:], sc[:, 1:2])
                        dve.scalar_tensor_tensor(out=exp_scale[:], in0=es[:, 0:1], scalar=float(HD) ** -0.5,
                                                 in1=es[:, 0:1], op0=ALU.mult, op1=ALU.mult)

                    @block.scalar
                    def _(act):
                        for i, (w, wd) in enumerate(((stg, wqk), (stgv, wv))):
                            act.wait_ge(p0_sc, 3 * (i + 1))
                            for c in range(C):
                                nc.scalar.activation(wd[:, 0, c, :], w[:, c, :], ACT.Copy, scale=sc[:, i:i + 1]).then_inc(p0_hi, 1)

            end_phase()

            with ExitStack() as p1:
                xt = sb(p1, "xt", [P, T, H])
                xnT = sb(p1, "xnT", [P, 2, C, S], F16)
                qk_hl = sb(p1, "qk_hl", [P, 2, 2, 2, S], F16)
                qs = sb(p1, "qs", [P, RING, S], F16)
                ks = sb(p1, "ks", [P, RING, S], F16)
                v_sb = sb(p1, "v_sb", [P, T, HEADS_A, V1], F16)
                vg = sb(p1, "vg", [P, 2, T, GH * V1], F16)
                e32 = sb(p1, "e32", [P, 2, 2, S])
                ehi = sb(p1, "ehi", [P, 2, T, S], F16)
                elo = sb(p1, "elo", [P, 2, T, S], F16)
                stage = sb(p1, "stage", [P, 2, 512])
                nmax = sb(p1, "nmax", [P, 2, T])
                nrow = sb(p1, "nrow", [P, 2, T, 2], F16)
                ident16 = sb(p1, "ident16", [P, P], F16)
                sums = sb(p1, "sums", [P, 2, T, V1])
                rsum = sb(p1, "rsum", [P, 2, T])
                ctx = sb(p1, "ctx", [P, 2, T, P])
                st6 = sb(p1, "st6", [P, 2, 2, 6])
                mv = sb(p1, "mv", [P, 2, 2])
                rstd = sb(p1, "rstd", [P, 2])
                mhalf = sb(p1, "mhalf", [P, 1])

                st_ps = ps(p1, "st_ps", [P, 2, 2, S])
                ring_ps = ps(p1, "ring_ps", [P, 2, S])
                ctx_ps = ps(p1, "ctx_ps", [P, 512])
                proj_ps = ps(p1, "proj_ps", [P, 512])
                ctx_v = ctx_ps[:, 0:T * V1].rearrange("p (t v) -> p t v", t=T)

                x_in = [sem(f"x_in{t}") for t in range(T)]
                stack_in = [sem(f"stack_in{r}") for r in range(RING)]
                vg_in = [sem(f"vg_in{i}") for i in range(2)]
                ctx_out = [sem(f"ctx_out{i}") for i in range(2)]
                (ring_full, ring_free, st_full, e32_done, ehi_done, elo_dve, elo_pool, pv_done, sums_done, csum_done,
                 rsum_done, ctx_done, row_hi, row_done, row_in, proj_full, proj_free, hi_done, split_done,
                 stat_done, aggr_done, var_done, rstd_done, xn_done, const_done) = (sem(n) for n in (
                    "ring_full", "ring_free", "st_full", "e32_done", "ehi_done", "elo_dve", "elo_pool", "pv_done",
                    "sums_done", "csum_done", "rsum_done", "ctx_done", "row_hi", "row_done", "row_in",
                    "proj_full", "proj_free", "hi_done", "split_done", "stat_done", "aggr_done",
                    "var_done", "rstd_done", "xn_done", "const_done"))

                def use_max(h, c):
                    return 5 * h + (c + 1 if c > 1 else c)

                def use_row(h):
                    return 5 * h + 7

                def over(r):
                    return r + 1 if isinstance(r, int) and r < 2 else r

                def unit_T(b, i):
                    return 32 * b + i

                def unit_QK(b, g, qk):
                    return 32 * b + (8 if isinstance(g, int) and g < 2 else 16) + 2 * g + qk

                def unit_V(b, i):
                    return 32 * b + 12 + i

                def live(h):
                    return not isinstance(h, int) or 0 <= h < TOT

                def leave(table, unit, k, q):
                    table.setdefault((k + q // 4, q % 4), []).insert(0, ("E",) + unit)
                    q = min(k * 4 + q + 1, 43)
                    table.setdefault((q // 4, q % 4), []).append(("S",) + unit)

                def spread(table, unit, k, quarters):
                    n = len(quarters) - 1
                    for i, q in enumerate(quarters[:-1]):
                        table.setdefault((k + q // 4, q % 4), []).append(unit + (24 * i // n, 24 * (i + 1) // n))
                    leave(table, unit, k, quarters[-1])

                def fills(gp, last_row):
                    t = {}
                    fast = [0, 1, 2, 3]
                    if gp is None:
                        for k, (g, qk) in ((3, (3, 0)), (5, (3, 1)), (7, (4, 0)), (9, (4, 1))):
                            spread(t, ("QK", 0, g, qk), k, list(range(8 if k < 9 else 7)))
                    elif gp == 2:
                        for k, qk in ((3, 0), (4, 1)):
                            spread(t, ("QK", 0, 3, qk), k, fast)
                        if not last_row:
                            for i in range(T):
                                t.setdefault((4 + i // 2, 2 * (i % 2)), []).append(("LN", i))
                                t.setdefault((4 + i // 2, 2 * (i % 2) + 1), []).append(("XN", i))
                            for i in range(2 * T):
                                t.setdefault((5 + (i + 2) // 4, (i + 2) % 4), []).append(("T", i))
                                leave(t, ("T", i), 5, i + 3)
                            for i, (g, qk) in enumerate(((-4, 0), (-4, 1), (-3, 0))):
                                spread(t, ("QK", 1, g, qk), 7, [4 * i + j for j in (4, 5, 6, 7)])
                    elif not last_row:
                        units = [("QK", 1, -5, 1)] + [("V", i) for i in range(2 * T)] + \
                                [("QK", 1, -4, 0), ("QK", 1, -4, 1)]
                        for i, u in enumerate(units):
                            q = 8 * (i // 3) + (0, 3, 6)[i % 3] - (i == 8)
                            spread(t, u, 3, [q, q + 1, q + 2])
                    return t

                def whole_phase(eng, prologue, pair):
                    prologue()
                    pair(0, 0, range(0, 3))
                    if B > 1:
                        with eng.Fori(0, B - 1) as b:
                            with eng.Fori(0, 2) as gp:
                                pair(b, gp, range(3, 11))
                            pair(b, 2, range(3, 11))
                            pair(b, 3, range(3, 11))
                    with eng.Fori(0, 2) as gp:
                        pair(B - 1, gp, range(3, 11))
                    pair(B - 1, 2, range(3, 11), True)
                    pair(B - 1, 3, range(3, 11), True)

                with nc.Block() as block:
                    @block.sync
                    def _(sp):
                        def load_x(b, t):
                            wait(sp, proj_full, unit_T(b, 2 * t + 2) - 32)
                            sp.dma_start(xt[:, t, :], x_t[b, t]).then_inc(x_in[t], 16)

                        def stacks(b, gp, o):
                            m = 8 * b + 2 * gp + o
                            if isinstance(m, int) and not m * GH < TOT:
                                return
                            bb, g = (b + 1, 2 * gp + o - G) if isinstance(gp, int) and 2 * gp + o >= G else (b, 2 * gp + o)
                            sp.wait_ge(split_done, unit_QK(bb, g, 1) + 1)
                            for i in range(GH):
                                r = (o % 2) * GH + i
                                wait(sp, st_full, 2 * (GH * m + i - RING + 1))
                                for tile, qk, parts in ((qs, 0, (0, 1, 0)), (ks, 1, (0, 0, 1))):
                                    for j, part in enumerate(parts):
                                        sp.dma_start(tile[HD * j:HD * j + HD, r, :],
                                                     qk_hl[HD * i:HD * i + HD, o % 2, qk, part, :]).then_inc(stack_in[r], 16)

                        def values(b, gp, o):
                            m = 8 * b + 2 * gp + o
                            if isinstance(m, int) and not m * GH < TOT:
                                return
                            bb, g = (b + 1, 2 * gp + o - G) if isinstance(gp, int) and 2 * gp + o >= G else (b, 2 * gp + o)
                            wait_apart(sp, split_done, unit_V(bb, 2 * T))
                            wait(sp, pv_done, 2 * GH * (m - 1))
                            sp.dma_start(vg[:, o % 2].rearrange("p t (h v) -> p t h v", h=GH),
                                         v_sb[:, :, bass.ds(GH * g, GH), :]).then_inc(vg_in[o % 2], 16)

                        def context(b, gp, o):
                            m = 8 * b + 2 * gp + o
                            sp.wait_ge(ctx_done, GH * (m + 1))
                            sp.dma_start(ctx_d[m].rearrange("t p d -> p t d"), ctx[:, o]).then_inc(ctx_out[o], 16)

                        def prologue():
                            for t in range(T):
                                load_x(0, t)
                            for o in range(2):
                                stacks(0, 0, o)
                                values(0, 0, o)

                        def pair(b, gp, slots, last_row=False):
                            for k in slots:
                                if k == 3 and isinstance(gp, int) and gp == 2 and not last_row:
                                    for t in range(T):
                                        load_x(b + 1, t)
                                if k == 4:
                                    stacks(b, gp, 2)
                                if k == 5 and not (isinstance(gp, int) and gp == 3):
                                    values(b, gp, 2)
                                if k == 7:
                                    context(b, gp, 0)
                                if k == 8:
                                    if isinstance(gp, int) and gp == 3:
                                        values(b, gp, 2)
                                    stacks(b, gp, 3)
                                if k == 9:
                                    values(b, gp, 3)
                                if k == 10:
                                    context(b, gp, 1)

                        whole_phase(sp, prologue, pair)
                        for i in range(2):
                            sp.wait_ge(ctx_out[i], 16 * B * G // 2)

                    @block.tensor
                    def _(pe):
                        def max_scores(p, k, c):
                            h = 8 * p + k
                            if not live(h):
                                return
                            r = k % RING
                            if c == 0:
                                pe.wait_ge(stack_in[r], 96 * (p + k // RING + 1))
                            wait(pe, ring_free, over(use_max(h, c) - 2) if live(h - 1) or c else 0)
                            pe.matmul(ring_ps[:, use_max(k, c) % 2, :], qs[0:3 * HD, r, P * c:P * c + P],
                                      ks[0:3 * HD, r, :], start=True, stop=True).then_inc(ring_full, 1)

                        def max_rows(p, k):
                            h = 8 * p + k
                            if not live(h):
                                return
                            pe.wait_ge(row_done, h + 1)
                            wait(pe, ring_free, min(use_row(h) - 2, 5 * TOT - 1) if isinstance(h, int) else use_row(h) - 2)
                            rows = ring_ps[:, use_row(k) % 2, :].bitcast(F16)
                            for c in range(T):
                                mm = pe.transpose(rows[0:2, P * c:P * c + P], nrow[:, k % 2, c, :], ident16[:])
                            mm.then_inc(ring_full, 1)

                        def scores(p, k, c):
                            h, r = 8 * p + k, k % RING
                            if not live(h):
                                return
                            if c == 0:
                                pe.wait_ge(row_in, h + 1)
                            if c % 2 == 0:
                                wait(pe, ehi_done, 2 * h - 1 + c // 2 if live(h - 1) else 0)
                            mm = pe.matmul(st_ps[:, c // 2, c % 2, :], ks[0:3 * HD + 2, r, P * c:P * c + P],
                                           qs[0:3 * HD + 2, r, :], start=True, stop=True)
                            if c % 2:
                                mm.then_inc(st_full, 1)

                        def weighted(p, k, c):
                            h, par, i = 8 * p + k, (k // GH) % 2, k % GH
                            if not live(h):
                                return
                            if c == 0:
                                wait(pe, sums_done, h)
                                if i == 0:
                                    pe.wait_ge(vg_in[par], 16 * (p + k // RING + 1))
                            if c % 2 == 0:
                                pe.wait_ge(ehi_done, 2 * h + 1 + c // 2)
                                pe.wait_ge(elo_pool if c else elo_dve, h + 1)
                            for t in range(T):
                                pe.matmul(ctx_v[:, t, :], ehi[:, k % 2, c, P * t:P * t + P],
                                          vg[:, par, c, V1 * i:V1 * i + V1], start=(c == 0 and t == 0), stop=False,
                                          skip_group_check=True)
                                mm = pe.matmul(ctx_v[:, t, 0:HD + 1], elo[:, k % 2, c, P * t:P * t + P],
                                               vg[:, par, c, V1 * i:V1 * i + HD + 1], start=False,
                                               stop=(c == T - 1), skip_group_check=True)
                            if c % 2:
                                mm.then_inc(pv_done, 1)

                        def qk_part(bb, g, qk, a, z):
                            if a == 0:
                                wait(pe, proj_free, unit_QK(bb, g, qk))
                                if isinstance(g, int) and g == 0 and qk == 0:
                                    pe.wait_ge(split_done, unit_T(bb, 2 * T))
                            for n in range(a, z):
                                c, (wp, xp) = n // 3, ((0, 0), (0, 1), (1, 0))[n % 3]
                                mm = pe.matmul(proj_ps[:], wqk[:, wp, c, bass.ds(H * qk + P * g, P)], xnT[:, xp, c, :],
                                               start=(n == 0), stop=(n == 23))
                            if z == 24:
                                mm.then_inc(proj_full, 1)

                        def v_part(bb, i, a, z):
                            if a == 0:
                                wait(pe, proj_free, unit_V(bb, i))
                            t, half = i // 2, i % 2
                            for n in range(a, z):
                                c, (xp, wp) = n // 3, ((0, 0), (0, 1), (1, 0))[n % 3]
                                mm = pe.matmul(proj_ps[:], xnT[:, xp, c, P * t:P * t + P],
                                               wv[:, wp, c, S * half:S * half + S], start=(n == 0), stop=(n == 23))
                            if z == 24:
                                mm.then_inc(proj_full, 1)

                        def turn(bb, i):
                            wait(pe, proj_free, unit_T(bb, i))
                            if i % 2 == 0:
                                pe.wait_ge(xn_done, T * bb + i // 2 + 1)
                            for c in range(4):
                                h0 = P * (4 * (i % 2) + c)
                                mm = pe.transpose(proj_ps[:, P * c:P * c + P], xt[:, i // 2, h0:h0 + P], ident[:])
                            mm.then_inc(proj_full, 1)

                        def prologue():
                            for i in range(2 * T):
                                turn(0, i)
                            for g in range(2):
                                for qk in range(2):
                                    qk_part(0, g, qk, 0, 24)
                            for i in range(2 * T):
                                v_part(0, i, 0, 24)
                            for qk in range(2):
                                qk_part(0, 2, qk, 0, 24)
                            pe.wait_ge(const_done, 4)
                            for c in range(T):
                                max_scores(0, 0, c)
                            for c in range(T):
                                max_scores(0, 1, c)
                                if c == 1:
                                    max_rows(0, 0)

                        def pair(b, gp, slots, last_row=False):
                            work = fills(gp if isinstance(gp, int) else None, last_row)
                            p = 4 * b + gp
                            for k in slots:
                                for c in range(T):
                                    max_scores(p, k + 2, c)
                                    if c == 1:
                                        max_rows(p, k + 1)
                                    scores(p, k, c)
                                    for f in work.get((k, c), []):
                                        if f[0] == "T":
                                            turn(b + 1, f[1])
                                        elif f[0] == "V":
                                            v_part(b + 1, *f[1:])
                                        elif f[0] == "QK":
                                            qk_part(b + f[1], 2 * gp + f[2], *f[3:])
                                    weighted(p, k - 2, c)

                        whole_phase(pe, prologue, pair)

                    @block.scalar
                    def _(act):
                        def exps(p, k, half):
                            h = 8 * p + k
                            if not live(h):
                                return
                            act.wait_ge(st_full, 2 * h + half + 1)
                            wait(act, elo_pool if half else elo_dve, h)
                            nc.scalar.activation(e32[:, half], st_ps[:, half], ACT.Exp, scale=exp_scale[:, 0:1]).then_inc(e32_done, 1)
                            wait(act, pv_done, 2 * (h - 2) + half + 1)
                            nc.scalar.activation(ehi[:, k % 2, 2 * half:2 * half + 2, :], st_ps[:, half], ACT.Exp,
                                                 scale=exp_scale[:, 0:1]).then_inc(ehi_done, 1)

                        def leave_proj(u, par, bias=None):
                            act.wait_ge(proj_full, u + 1)
                            wait(act, split_done, u - 1)
                            if bias is None:
                                nc.scalar.activation(stage[:, par], proj_ps[:], ACT.Copy).then_inc(proj_free, 1)
                            else:
                                nc.scalar.activation(stage[:, par], proj_ps[:], ACT.Identity, bias=bias).then_inc(proj_free, 1)

                        def leave_T(bb, i):
                            leave_proj(unit_T(bb, i), i % 2)

                        def leave_V(bb, i):
                            leave_proj(unit_V(bb, i), i % 2)

                        def leave_QK(bb, g, qk):
                            leave_proj(unit_QK(bb, g, qk), qk, bqk[:, bass.ds(8 * qk + g, 1)])

                        def prologue():
                            for i in range(2 * T):
                                leave_T(0, i)
                            for g in range(2):
                                for qk in range(2):
                                    leave_QK(0, g, qk)
                            for i in range(2 * T):
                                leave_V(0, i)
                            for qk in range(2):
                                leave_QK(0, 2, qk)

                        def pair(b, gp, slots, last_row=False):
                            work = fills(gp if isinstance(gp, int) else None, last_row)
                            p = 4 * b + gp
                            for k in slots:
                                for c in range(T):
                                    for f in work.get((k, c), []):
                                        if f[0] == "E":
                                            if f[1] == "T":
                                                leave_T(b + 1, f[2])
                                            elif f[1] == "QK":
                                                leave_QK(b + f[2], 2 * gp + f[3], f[4])
                                            else:
                                                leave_V(b + 1, f[2])
                                    if c % 2:
                                        exps(p, k, c // 2)

                        whole_phase(act, prologue, pair)

                    @block.vector
                    def _(dve):
                        def max_of(p, k, c):
                            h = 8 * p + k
                            if not live(h):
                                return
                            dve.wait_ge(ring_full, over(use_max(h, c)))
                            dve.tensor_reduce(nmax[:, k % 2, c:c + 1], ring_ps[:, use_max(k, c) % 2, :], AX.X, ALU.max,
                                              negate=True).then_inc(ring_free, 1)

                        def row_parts(p, k):
                            h = 8 * p + k
                            if not live(h):
                                return
                            dve.wait_ge(ring_free, use_max(h, T - 1))
                            dve.tensor_scalar(nrow[:, k % 2, :, 0], nmax[:, k % 2, :], 1.0 / ONES_ROW, None,
                                              ALU.mult).then_inc(row_hi, 1)
                            dve.wait_ge(row_hi, h + 1)
                            dve.scalar_tensor_tensor(out=nrow[:, k % 2, :, 1], in0=nmax[:, k % 2, :], scalar=1.0 / ONES_ROW,
                                                     in1=nrow[:, k % 2, :, 0], op0=ALU.mult, op1=ALU.subtract).then_inc(row_done, 1)

                        def row_stack(p, k):
                            h = 8 * p + k
                            if not live(h):
                                return
                            dve.wait_ge(ring_full, min(use_row(h), 5 * TOT) if isinstance(h, int) else use_row(h))
                            rows = ring_ps[:, use_row(k) % 2, :].bitcast(F16)
                            dve.tensor_copy(qs[3 * HD:3 * HD + 2, k % RING, :], rows[0:2, 0:S]).then_inc(row_in, 1)
                            dve.wait_ge(row_in, h + 1)
                            dve.sem_inc(ring_free, 1)

                        def lo_exps(p, k):
                            h = 8 * p + k
                            if not live(h):
                                return
                            dve.wait_ge(ehi_done, 2 * h + 1)
                            dve.tensor_tensor(elo[:, k % 2, 0:2, :], e32[:, 0], ehi[:, k % 2, 0:2, :],
                                              ALU.subtract).then_inc(elo_dve, 1)

                        def leave_ctx(p, k):
                            h = 8 * p + k
                            if not live(h):
                                return
                            dve.wait_ge(pv_done, 2 * h + 2)
                            dve.reciprocal(rsum[:, k % 2], ctx_v[:, :, HD]).then_inc(rsum_done, 1)
                            dve.tensor_copy(sums[:, k % 2], ctx_v[:]).then_inc(sums_done, 1)

                        def split_T(bb, i):
                            dve.wait_ge(proj_free, unit_T(bb, i) + 1)
                            t, c0 = i // 2, 4 * (i % 2)
                            dve.tensor_copy(xnT[:, 0, c0:c0 + 4, P * t:P * t + P],
                                            stage[:, i % 2].rearrange("p (c n) -> p c n", c=4)).then_inc(hi_done, 1)
                            wait(dve, split_done, unit_T(bb, i))
                            dve.wait_ge(hi_done, unit_T(bb, i) + 1)
                            dve.tensor_tensor(xnT[:, 1, c0:c0 + 4, P * t:P * t + P],
                                              stage[:, i % 2].rearrange("p (c n) -> p c n", c=4),
                                              xnT[:, 0, c0:c0 + 4, P * t:P * t + P], ALU.subtract).then_inc(split_done, 1)

                        def hi_QK(bb, gp, o, qk):
                            dve.wait_ge(proj_free, unit_QK(bb, 2 * gp + o, qk) + 1)
                            for i in range(GH):
                                wait(dve, stack_in[(o % 2) * GH + i], 96 * (4 * bb + gp + o // 2))
                            dve.tensor_copy(qk_hl[:, o % 2, qk, 0, :], stage[:, qk]).then_inc(hi_done, 1)

                        def hi_V(bb, i):
                            dve.wait_ge(proj_free, unit_V(bb, i) + 1)
                            if i == 0:
                                wait(dve, vg_in[0], 64 * bb)
                                wait(dve, vg_in[1], 64 * bb)
                            dve.tensor_copy(v_sb[:, i // 2, 16 * (i % 2):16 * (i % 2) + 16, 0:HD],
                                            stage[:, i % 2].rearrange("p (h d) -> p h d", d=HD)).then_inc(hi_done, 1)

                        def stats(bb, t):
                            dve.wait_ge(x_in[t], 16 * (bb + 1))
                            wait(dve, xn_done, T * bb + t - 1)
                            for i in range(2):
                                dve.bn_stats(st6[:, t % 2, i, :], xt[:, t, S * i:S * i + S]).then_inc(stat_done, 1)
                            wait_apart(dve, stat_done, 2 * (T * bb + t + 1))
                            dve.bn_aggr(mv[:, t % 2], st6[:, t % 2].rearrange("p a b -> p (a b)")).then_inc(aggr_done, 1)

                        def normalise(bb, t):
                            dve.wait_ge(rstd_done, T * bb + t + 1)
                            dve.tensor_scalar(xt[:, t, :], xt[:, t, :], mv[:, t % 2, 0:1], rstd[:, t % 2:t % 2 + 1],
                                              ALU.subtract, ALU.mult).then_inc(xn_done, 1)

                        def prologue():
                            dve.memset(mhalf[:], -0.5).then_inc(const_done, 1)
                            for t in range(T):
                                stats(0, t)
                                if t:
                                    normalise(0, t - 1)
                            normalise(0, T - 1)
                            dve.memset(v_sb[:, :, :, HD:HD + 1], 1.0).then_inc(const_done, 1)
                            dve.tensor_copy(ident16[:], ident[:]).then_inc(const_done, 1)
                            for i in range(2 * T):
                                split_T(0, i)
                            for g in range(2):
                                for qk in range(2):
                                    hi_QK(0, 0, g, qk)
                            dve.memset(ks[3 * HD:3 * HD + 2], ONES_ROW).then_inc(const_done, 1)
                            for i in range(2 * T):
                                hi_V(0, i)
                            for qk in range(2):
                                hi_QK(0, 0, 2, qk)
                            for c in range(T):
                                max_of(0, 0, c)
                            row_parts(0, 0)
                            for c in range(T):
                                max_of(0, 1, c)
                                if c == 1:
                                    row_stack(0, 0)
                            row_parts(0, 1)

                        def pair(b, gp, slots, last_row=False):
                            work = fills(gp if isinstance(gp, int) else None, last_row)
                            p = 4 * b + gp
                            for k in slots:
                                for c in range(T):
                                    if c == 0:
                                        leave_ctx(p, k - 3)
                                    max_of(p, k + 2, c)
                                    if c == 1:
                                        row_stack(p, k + 1)
                                    if c == T - 1:
                                        row_parts(p, k + 2)
                                    if c == 0:
                                        lo_exps(p, k - 1)
                                    for f in work.get((k, c), []):
                                        if f[0] == "LN":
                                            stats(b + 1, f[1])
                                        elif f[0] == "XN":
                                            normalise(b + 1, f[1])
                                        elif f[0] == "S":
                                            if f[1] == "T":
                                                split_T(b + 1, f[2])
                                            elif f[1] == "QK":
                                                hi_QK(b + f[2], gp, f[3], f[4])
                                            else:
                                                hi_V(b + 1, f[2])

                        whole_phase(dve, prologue, pair)

                    @block.gpsimd
                    def _(pool):
                        def lo_exps(p, k):
                            h = 8 * p + k
                            if not live(h):
                                return
                            pool.wait_ge(ehi_done, 2 * h + 2)
                            nc.gpsimd.tensor_tensor(elo[:, k % 2, 2:4, :], e32[:, 1], ehi[:, k % 2, 2:4, :],
                                                    ALU.subtract).then_inc(elo_pool, 1)

                        def normalise(p, k):
                            h, par, i = 8 * p + k, (k // GH) % 2, k % GH
                            if not live(h):
                                return
                            pool.wait_ge(sums_done, h + 1)
                            nc.gpsimd.tensor_tensor(sums[:, k % 2, :, 0:HD], sums[:, k % 2, :, 0:HD], sums[:, k % 2, :, HD + 1:V1],
                                                    ALU.add).then_inc(csum_done, 1)
                            if i == 0:
                                wait(pool, ctx_out[par], 16 * (p + k // RING))
                            pool.wait_ge(rsum_done, h + 1)
                            pool.wait_ge(csum_done, h + 1)
                            nc.gpsimd.tensor_tensor(ctx[:, par, :, HD * i:HD * i + HD], sums[:, k % 2, :, 0:HD],
                                                    rsum[:, k % 2].unsqueeze(2).to_broadcast([P, T, HD]),
                                                    ALU.mult).then_inc(ctx_done, 1)

                        def inv_deviation(bb, t):
                            n = T * bb + t
                            wait_apart(pool, aggr_done, n + 1)
                            nc.gpsimd.tensor_scalar(rstd[:, t % 2:t % 2 + 1], mv[:, t % 2, 1:2], LN_EPS, None, ALU.add).then_inc(var_done, 1)
                            pool.wait_ge(var_done, n + 1)
                            nc.gpsimd.tensor_tensor(rstd[:, t % 2:t % 2 + 1], rstd[:, t % 2:t % 2 + 1], mhalf[:], ALU.pow).then_inc(rstd_done, 1)

                        def lo_QK(bb, gp, o, qk):
                            pool.wait_ge(hi_done, unit_QK(bb, 2 * gp + o, qk) + 1)
                            nc.gpsimd.tensor_tensor(qk_hl[:, o % 2, qk, 1, :], stage[:, qk], qk_hl[:, o % 2, qk, 0, :],
                                                    ALU.subtract).then_inc(split_done, 1)

                        def lo_V(bb, i):
                            pool.wait_ge(hi_done, unit_V(bb, i) + 1)
                            hs = slice(16 * (i % 2), 16 * (i % 2) + 16)
                            nc.gpsimd.tensor_tensor(v_sb[:, i // 2, hs, HD + 1:V1], stage[:, i % 2].rearrange("p (h d) -> p h d", d=HD),
                                                    v_sb[:, i // 2, hs, 0:HD], ALU.subtract).then_inc(split_done, 1)

                        def prologue():
                            for t in range(T):
                                inv_deviation(0, t)
                            for g in range(2):
                                for qk in range(2):
                                    lo_QK(0, 0, g, qk)
                            for i in range(2 * T):
                                lo_V(0, i)
                            for qk in range(2):
                                lo_QK(0, 0, 2, qk)

                        def pair(b, gp, slots, last_row=False):
                            work = fills(gp if isinstance(gp, int) else None, last_row)
                            p = 4 * b + gp
                            for k in slots:
                                for c in range(T):
                                    if c == 0:
                                        normalise(p, k - 3)
                                    if c == 1:
                                        lo_exps(p, k - 1)
                                    for f in work.get((k, c), []):
                                        if f[0] == "LN":
                                            inv_deviation(b + 1, f[1])
                                        elif f[0] == "S":
                                            if f[1] == "QK":
                                                lo_QK(b + f[2], gp, f[3], f[4])
                                            elif f[1] == "V":
                                                lo_V(b + 1, f[2])

                        whole_phase(pool, prologue, pair)

        end_phase()

        with ExitStack() as p234:
            hit_rows = sb(p234, "hit_rows", [NC, H], F16)
            centT = sb(p234, "centT", [P, 2, C, NC], F16)
            fbias = sb(p234, "fbias", [P, H])
            hits = sb(p234, "hits", [P, 2, NC])
            ones = sb(p234, "ones", [P, P])
            qsel = sb(p234, "qsel", [P, 2, B * T])
            e_w = sb(p234, "e_w", [P, 3])
            cent_scale = sb(p234, "cent_scale", [P, 1])
            mhalf = sb(p234, "mhalf2", [P, 1])

            with ExitStack() as p2:
                stg = sb(p2, "stg2", [P, C, H])
                stgw = sb(p2, "stgw", [P, C, H])
                wo = sb(p2, "wo", [P, 2, C, H], F16)
                wT = sb(p2, "wT", [P, 2, C, H], F16)
                cst = sb(p2, "cst", [NC, H])
                asg = sb(p2, "asg", [NC, H], I32)
                asgf = sb(p2, "asgf", [NC, H])
                cid = sb(p2, "cid", [NC, 1], I32)
                cidf = sb(p2, "cidf", [NC, 1])
                mx, m1, m2, sc = (sb(p2, n, [P, 3]) for n in ("mx2", "m12", "m22", "sc2"))
                bv = sb(p2, "bv", [P, H])
                obias = sb(p2, "obias", [P, H])
                inv_o = sb(p2, "inv_o", [P, 1])
                ct = sb(p2, "ct", [P, T, H])
                xb = sb(p2, "xb", [P, T, H])
                cT = sb(p2, "cT", [P, 2, 2, C, P], F16)
                hit = HitTiles(sb, p2, "2")
                cT_ps = ps(p2, "cT_ps", [P, 2, 512])
                o_ps = ps(p2, "o_ps", [P, 2, 512])
                x_ps = ps(p2, "x_ps", [P, 2, 512])
                c_ps = ps(p2, "c_ps", [P, 512])
                (row_in2, half_max, fw_in, ct_in2, max2, all2, sc2, wo_hi, wo_lo, w_turned, w_hi, w_lo, c_turned, c_hi,
                 c_lo, misc2, inv2, cx_done, xb_done, cT_full, cT_hi, cT_lo, o_full, x1_done, cid_done) = (
                    sem(n) for n in ("row_in2", "half_max", "fw_in", "ct_in2", "max2", "all2", "sc2", "wo_hi", "wo_lo",
                                     "w_turned", "w_hi", "w_lo", "c_turned", "c_hi", "c_lo", "misc2", "inv2",
                                     "cx_done", "xb_done", "cT_full", "cT_hi", "cT_lo", "o_full", "x1_done",
                                     "cid_done"))
                wT_out = sem("wT_out")
                ow_in = [sem(f"ow_in{i}") for i in range(2)]
                tile_in = [sem(f"tile_in{t}") for t in range(T)]
                store2 = [sem(f"store2_{t}") for t in range(T)]
                hs = HitSems(sem, "2")

                def steps(eng, step, first=3):
                    for n in range(-1, first):
                        step(0, n)
                    if B > 1:
                        with eng.Fori(0, B - 1) as b:
                            for k in range(first, first + T):
                                step(b, k)
                    for k in range(first, first + T):
                        step(B - 1, k)

                def tile(b, k):
                    n = T * b + k
                    return not isinstance(n, int) or 0 <= n < T * B, n

                with nc.Block() as block:
                    @block.sync
                    def _(sp):
                        for i in range(2):
                            sp.dma_start(stg[:, 4 * i:4 * i + 4], ow.rearrange("(c p) n -> p c n", p=P)[:, 4 * i:4 * i + 4]).then_inc(ow_in[i], 16)
                        sp.dma_start(cst[:], cent).then_inc(ct_in2, 16)
                        sp.dma_start(bv[:], qkvb[2 * H:3 * H].partition_broadcast(P)).then_inc(row_in2, 16)
                        sp.dma_start(obias[:], ob.partition_broadcast(P)).then_inc(row_in2, 16)
                        sp.dma_start(fbias[:], fb.partition_broadcast(P)).then_inc(row_in2, 16)
                        sp.dma_start(asg[:], assign.partition_broadcast(NC)).then_inc(row_in2, 16)
                        sp.dma_start(stgw[:], fw.rearrange("(o p) i -> p o i", p=P)).then_inc(fw_in, 16)

                        def load(b, k):
                            ok, n = tile(b, k)
                            if not ok:
                                return
                            t = k % T
                            wait(sp, store2[t], 32 * (b + k // T))
                            bb = b + k // T
                            sp.dma_start(ct[:, t].rearrange("p (g d) -> p g d", d=P),
                                         ctx_t[bb, :, t].rearrange("g p d -> p g d")).then_inc(tile_in[t], 16)
                            sp.dma_start(xb[:, t], x_t[bb, t]).then_inc(tile_in[t], 16)

                        def store(b, k):
                            ok, n = tile(b, k)
                            if not ok:
                                return
                            sp.wait_ge(x1_done, 2 * n + 2)
                            sp.dma_start(x1_d[n], ct[:, k % T]).then_inc(store2[k % T], 16)
                            sp.wait_ge(hs.lo, 2 * n + 2)
                            sp.dma_start(xT1_d[n], hit.xT[:, k % 2]).then_inc(store2[k % T], 16)

                        def step(b, k):
                            store(b, k - 2)
                            if not isinstance(b, int) or b > 0 or k + 2 >= T:
                                load(b, k + 2)

                        for t in range(T):
                            load(0, t)
                        sp.wait_ge(w_lo, 2 * C)
                        sp.dma_start(wT_d, wT[:]).then_inc(wT_out, 16)
                        steps(sp, step, 2)
                        sp.wait_ge(wT_out, 16)
                        for t in range(T):
                            sp.wait_ge(store2[t], 32 * B)

                    @block.tensor
                    def _(pe):
                        pe.wait_ge(ct_in2, 16)
                        for c in range(C):
                            mm = pe.transpose(c_ps[:, NC * c:NC * c + NC], cst[:, P * c:P * c + P], ident[0:NC, 0:NC])
                        mm.then_inc(c_turned, 1)
                        pe.wait_ge(fw_in, 16)
                        for i in range(2 * C):
                            c, half = i // 2, i % 2
                            wait(pe, w_lo, i - 1)
                            for o in range(4):
                                mm = pe.transpose(cT_ps[:, i % 2, P * o:P * o + P], stgw[:, 4 * half + o, P * c:P * c + P], ident[:])
                            mm.then_inc(w_turned, 1)

                        def turn_context(b, k):
                            ok, n = tile(b, k)
                            if not ok:
                                return
                            pe.wait_ge(cx_done, n + 1)
                            if isinstance(n, int) and n == 0:
                                pe.wait_ge(w_lo, 2 * C)
                            for half in range(2):
                                wait(pe, cT_lo, 2 * n - 1 + half if not isinstance(n, int) or n > 0 else 0)
                                for c in range(4):
                                    h0 = P * (4 * half + c)
                                    mm = pe.transpose(cT_ps[:, half, P * c:P * c + P], ct[:, k % T, h0:h0 + P], ident[:])
                                mm.then_inc(cT_full, 1)

                        def project(b, k):
                            ok, n = tile(b, k)
                            if not ok:
                                return
                            pe.wait_ge(cT_lo, 2 * n + 2)
                            if isinstance(n, int) and n == 0:
                                pe.wait_ge(wo_lo, C)
                            for half in range(2):
                                wait(pe, x1_done, 2 * n - 1 + half if not isinstance(n, int) or n > 0 else 0)
                                for i in range(24):
                                    c, (xp, wp) = i // 3, ((0, 0), (0, 1), (1, 0))[i % 3]
                                    mm = pe.matmul(o_ps[:, half, :], cT[:, k % 2, xp, c, :], wo[:, wp, c, 512 * half:512 * half + 512],
                                                   start=(i == 0), stop=(i == 23))
                                mm.then_inc(o_full, 1)

                        def step(b, k):
                            turn_context(b, k + 1)
                            if tile(b, k - 2)[0]:
                                hit_turn(pe, hs, hit, x_ps, xb[:, (k - 2) % T], ident, tile(b, k - 2)[1], k % 2)
                            project(b, k)
                            if tile(b, k - 2)[0]:
                                hit_logits(pe, hs, hit, c_ps, centT, tile(b, k - 2)[1], k % 2)

                        pe.wait_ge(c_lo, 1)
                        steps(pe, step)

                    @block.scalar
                    def _(act):
                        act.wait_ge(sc2, 3)
                        for c in range(C):
                            nc.scalar.activation(wo[:, 0, c, :], stg[:, c, :], ACT.Copy, scale=sc[:, 0:1]).then_inc(wo_hi, 1)
                        act.wait_ge(sc2, 6)
                        act.wait_ge(c_turned, 1)
                        nc.scalar.activation(centT[:, 0], c_ps[:, 0:C * NC].rearrange("p (c n) -> p c n", c=C), ACT.Copy,
                                             scale=sc[:, 1:2]).then_inc(c_hi, 1)
                        act.wait_ge(sc2, 9)
                        for i in range(2 * C):
                            act.wait_ge(w_turned, i + 1)
                            nc.scalar.activation(wT[:, 0, i // 2, 512 * (i % 2):512 * (i % 2) + 512], cT_ps[:, i % 2, :], ACT.Copy,
                                                 scale=sc[:, 2:3]).then_inc(w_hi, 1)

                        def hi_context(b, k):
                            ok, n = tile(b, k)
                            if not ok:
                                return
                            wait(act, o_full, 2 * n - 2)
                            for half in range(2):
                                act.wait_ge(cT_full, 2 * n + half + 1)
                                nc.scalar.activation(cT[:, k % 2, 0, 4 * half:4 * half + 4, :],
                                                     cT_ps[:, half, :].rearrange("p (c n) -> p c n", c=4), ACT.Copy).then_inc(cT_hi, 1)

                        def step(b, k):
                            hi_context(b, k + 1)
                            if tile(b, k - 2)[0]:
                                hit_hi(act, nc, hs, hit, x_ps, tile(b, k - 2)[1], k % 2, store2, k - 2, b)
                                hit_exp(act, nc, hs, hit, c_ps, cent_scale, tile(b, k - 2)[1], k % 2)

                        steps(act, step)

                    @block.vector
                    def _(dve):
                        dve.memset(m1[:], 0.0).then_inc(misc2, 1)
                        dve.memset(mhalf[:], -0.5).then_inc(misc2, 1)
                        dve.memset(hits[:], 0.0).then_inc(misc2, 1)
                        dve.memset(ones[:], 1.0).then_inc(misc2, 1)
                        dve.wait_ge(misc2, 4)
                        for i in range(2):
                            dve.wait_ge(ow_in[i], 16)
                            dve.tensor_reduce(mx[:, i:i + 1], stg[:, 4 * i:4 * i + 4], AX.XY, ALU.max, apply_absolute_value=True).then_inc(half_max, 1)
                        dve.wait_ge(half_max, 2)
                        dve.tensor_reduce(m1[:, 0:1], mx[:, 0:2], AX.X, ALU.max).then_inc(max2, 1)
                        dve.wait_ge(all2, 1)
                        n = scale_from_absmax(dve, m2[:, 0:1], e_w[:, 0:1], sc[:, 0:1], sc2, 0)
                        for c in range(C):
                            dve.wait_ge(wo_hi, c + 1)
                            dve.scalar_tensor_tensor(out=wo[:, 1, c, :], in0=stg[:, c, :], scalar=sc[:, 0:1], in1=wo[:, 0, c, :],
                                                     op0=ALU.mult, op1=ALU.subtract).then_inc(wo_lo, 1)
                        dve.tensor_tensor(inv_o[:], e_w[:, 0:1], e_v[:], ALU.mult).then_inc(inv2, 1)
                        dve.wait_ge(ct_in2, 16)
                        dve.tensor_reduce(m1[0:NC, 1:2], cst[:], AX.X, ALU.max, apply_absolute_value=True).then_inc(max2, 1)
                        dve.wait_ge(all2, 2)
                        n = scale_from_absmax(dve, m2[:, 1:2], e_w[:, 1:2], sc[:, 1:2], sc2, n)
                        dve.tensor_scalar(cent_scale[:], e_w[:, 1:2], 1.0 / TEMPERATURE, None, ALU.mult).then_inc(inv2, 1)
                        dve.wait_ge(c_hi, 1)
                        dve.scalar_tensor_tensor(out=centT[:, 1], in0=c_ps[:, 0:C * NC].rearrange("p (c n) -> p c n", c=C),
                                                 scalar=sc[:, 1:2], in1=centT[:, 0], op0=ALU.mult, op1=ALU.subtract).then_inc(c_lo, 1)
                        dve.wait_ge(row_in2, 64)
                        dve.tensor_scalar(bv[:], bv[:], s_v[:, 0:1], None, ALU.mult).then_inc(inv2, 1)
                        dve.wait_ge(cid_done, 1)
                        dve.tensor_copy(asgf[:], asg[:]).then_inc(misc2, 1)
                        dve.tensor_copy(cidf[:], cid[:]).then_inc(misc2, 1)
                        dve.wait_ge(misc2, 6)
                        dve.tensor_scalar(hit_rows[:], asgf[:], cidf[:, 0:1], None, ALU.is_equal)
                        dve.wait_ge(fw_in, 16)
                        dve.tensor_reduce(m1[:, 2:3], stgw[:], AX.XY, ALU.max, apply_absolute_value=True).then_inc(max2, 1)
                        dve.wait_ge(all2, 3)
                        scale_from_absmax(dve, m2[:, 2:3], e_w[:, 2:3], sc[:, 2:3], sc2, n)
                        for i in range(2 * C):
                            cols = slice(512 * (i % 2), 512 * (i % 2) + 512)
                            dve.wait_ge(w_hi, i + 1)
                            dve.scalar_tensor_tensor(out=wT[:, 1, i // 2, cols], in0=cT_ps[:, i % 2, :], scalar=sc[:, 2:3],
                                                     in1=wT[:, 0, i // 2, cols], op0=ALU.mult, op1=ALU.subtract).then_inc(w_lo, 1)

                        def lo_context(b, k):
                            ok, n = tile(b, k)
                            if not ok:
                                return
                            for half in range(2):
                                dve.wait_ge(cT_hi, 2 * n + half + 1)
                                dve.tensor_tensor(cT[:, k % 2, 1, 4 * half:4 * half + 4, :],
                                                  cT_ps[:, half, :].rearrange("p (c n) -> p c n", c=4),
                                                  cT[:, k % 2, 0, 4 * half:4 * half + 4, :], ALU.subtract).then_inc(cT_lo, 1)

                        def residual(b, k):
                            ok, n = tile(b, k)
                            if not ok:
                                return
                            dve.wait_ge(xb_done, n + 1)
                            if isinstance(n, int) and n == 0:
                                dve.wait_ge(inv2, 3)
                            for half in range(2):
                                cols = slice(512 * half, 512 * half + 512)
                                dve.wait_ge(o_full, 2 * n + half + 1)
                                dve.scalar_tensor_tensor(out=ct[:, k % T, cols], in0=o_ps[:, half, :], scalar=inv_o[:, 0:1],
                                                         in1=xb[:, k % T, cols], op0=ALU.mult, op1=ALU.add).then_inc(x1_done, 1)
                            dve.wait_ge(x1_done, 2 * n + 2)
                            hit_stats(dve, hs, hit, ct[:, k % T], n, k % 2)

                        def step(b, k):
                            lo_context(b, k + 1)
                            if tile(b, k - 2)[0]:
                                hit_lo(dve, hs, hit, x_ps, tile(b, k - 2)[1], k % 2)
                            ok, n = tile(b, k - 1)
                            if ok:
                                hit_norm(dve, hs, hit, ct[:, (k - 1) % T], xb[:, (k - 1) % T], n, (k - 1) % 2)
                            residual(b, k)
                            if tile(b, k - 2)[0]:
                                hit_select(dve, hs, hit, c_ps, cent_scale, hits[:, 0], qsel[:, 0], tile(b, k - 2)[1], k % 2)

                        steps(dve, step)

                    @block.gpsimd
                    def _(pool):
                        nc.gpsimd.iota(cid[:], pattern=[[0, 1]], base=0, channel_multiplier=1).then_inc(cid_done, 1)
                        for i in range(3):
                            pool.wait_ge(max2, i + 1)
                            nc.gpsimd.partition_all_reduce(m2[:, i:i + 1], m1[:, i:i + 1], P, RMAX).then_inc(all2, 1)
                        pool.wait_ge(inv2, 3)

                        def biases(b, k):
                            ok, n = tile(b, k)
                            if not ok:
                                return
                            pool.wait_ge(tile_in[k % T], 32 * (b + k // T + 1))
                            nc.gpsimd.tensor_tensor(ct[:, k % T], ct[:, k % T], bv[:], ALU.add).then_inc(cx_done, 1)
                            nc.gpsimd.tensor_tensor(xb[:, k % T], xb[:, k % T], obias[:], ALU.add).then_inc(xb_done, 1)

                        def step(b, k):
                            biases(b, k + 1)
                            ok, n = tile(b, k - 1)
                            if ok:
                                hit_rstd(pool, nc, hs, hit, mhalf, n, (k - 1) % 2)

                        steps(pool, step)

            end_phase()

            D = H // HEADS_B
            with ExitStack() as p3:
                wm = sb(p3, "wm", [P, 2, C, H], F16)
                hrow = sb(p3, "hrow", [P, H])
                vb = sb(p3, "vb", [P, H])
                csel = sb(p3, "csel", [NC, P], F16)
                mask = sb(p3, "mask", [P, H], F16)
                alpha = sb(p3, "alpha", [P, HEADS_B])
                cq = sb(p3, "cq", [P, C])
                m3, e3, s3 = (sb(p3, n, [P, 2]) for n in ("m3", "e3", "s3"))
                sig_scale = sb(p3, "sig_scale", [P, 1])
                inv_f = sb(p3, "inv_f", [P, B * T])
                x2 = sb(p3, "x2", [P, 2, T, H])
                xn2 = sb(p3, "xn2", [P, T, H])
                xn3 = sb(p3, "xn3", [P, T, H])
                fxT = sb(p3, "fxT", [P, 2, 2, C, P], F16)
                xhT = sb(p3, "xhT", [P, 2, C, S], F16)
                yT = sb(p3, "yT", [P, 2, C, S], F16)
                vv = sb(p3, "vv", [P, 2, T, H], F16)
                a32 = sb(p3, "a32", [P, T, S])
                ahl = sb(p3, "ahl", [P, 2, T, S], F16)
                h3T = sb(p3, "h3T", [P, 2, 2, C, P], F16)
                ln2, ln3 = LnTiles(sb, p3, "_x2"), LnTiles(sb, p3, "_x3")
                c4 = sb(p3, "c4", [P, T, NC])
                cm, cs = sb(p3, "cm3", [P, T]), sb(p3, "cs3", [P, T])
                h4 = sb(p3, "h4", [P, 2, T, NC])
                t_ps = ps(p3, "t_ps", [P, 512])
                l_ps = ps(p3, "l_ps", [P, 512])
                f_ps = ps(p3, "f_ps", [P, 2, 512])
                s_ps = ps(p3, "s_ps", [P, 2, 512])
                pv_ps = ps(p3, "pv_ps", [P, 2, 2, D])

                names = ("bind_in", "p3c", "p3all", "p3sc", "csum3", "csel3", "mask_full", "mask3", "wm_done", "cT3", 
                         "xb3", "f_full", "x2_done", "n_full", "n_hi",
                         "n_lo", "v32", "v_hi", "v_lo", "s_full", "sig", "tri", "a_hi", "a_lo", "pv_full", "x3_done",
                         "h_full", "h_hi", "h_lo", "l_full", "lmax", "lsub", "lexp", "lsum", "lthr", "lhit", "lacc")
                q = {n: sem(n + "_3" if not n.endswith("3") else n) for n in names}
                w_in3 = sem("w_in3")
                ls2, ls3 = LnSems(sem, "_x2"), LnSems(sem, "_x3")
                x1_in = [sem(f"x1_in{t}") for t in range(T)]
                fxT_in = [sem(f"fxT_in{t}") for t in range(2)]
                x3_out = [sem(f"x3_out{t}") for t in range(T)]
                h3_out = [sem(f"h3_out{t}") for t in range(2)]

                def row(b):
                    return not isinstance(b, int) or 0 <= b < B

                def batch_rows(eng, step):
                    step(-1, 1)
                    step(0, 0)
                    if B > 2:
                        with eng.Fori(0, (B - 2) // 2) as r:
                            step(2 * r + 1, 1)
                            step(2 * r + 2, 0)
                    for b in range(max(1, 2 * ((B - 2) // 2) + 1), B + 1):
                        step(b, b % 2)

                with nc.Block() as block:
                    @block.sync
                    def _(sp):
                        sp.dma_start(fbias[:], fb.partition_broadcast(P)).then_inc(q["bind_in"], 16)
                        for dst, src in ((hrow, bvq), (xn2[:, 0], bvk), (vb, bvv)):
                            sp.dma_start(dst[:], src.rearrange("h d -> (h d)").partition_broadcast(P)).then_inc(q["bind_in"], 16)
                        sp.dma_start(wm[:], wT_d).then_inc(w_in3, 16)

                        def load_fxT(b, t):
                            if not row(b):
                                return
                            wait(sp, q["f_full"], 8 * b + 2 * t - 2)
                            sp.dma_start(fxT[:, t % 2], xT1_d[T * b + t]).then_inc(fxT_in[t % 2], 16)

                        def load_x1(b, par, t):
                            if not row(b):
                                return
                            wait_apart(sp, ls3.xn, T * (b - 2) + t + 1 if not isinstance(b, int) or b > 1 else 0)
                            wait(sp, x3_out[t], 16 * (b - 1))
                            sp.dma_start(x2[:, par, t], x1_d[T * b + t]).then_inc(x1_in[t], 16)

                        def step(b, par):
                            for t in range(2):
                                load_fxT(b + 1, t)
                            if row(b - 1):
                                for t in range(T):
                                    sp.wait_ge(q["x3_done"], 8 * b)
                                    sp.dma_start(x3_d[T * (b - 1) + t], x2[:, 1 - par, t]).then_inc(x3_out[t], 16)
                            for t in range(T):
                                if t >= 2:
                                    load_fxT(b + 1, t)
                                load_x1(b + 1, 1 - par, t)
                                if row(b - 1) and t >= 2:
                                    store_h(b - 1, t - 2)
                            if row(b - 1):
                                store_h(b - 1, 2)
                                store_h(b - 1, 3)

                        def store_h(b, t):
                            sp.wait_ge(q["h_lo"], 8 * b + 2 * t + 2)
                            sp.dma_start(xT3_d[T * b + t], h3T[:, t % 2]).then_inc(h3_out[t % 2], 16)

                        for t in range(2):
                            sp.sem_inc(h3_out[t], 16)
                        batch_rows(sp, step)
                        for t in range(T):
                            sp.wait_ge(x3_out[t], 16 * B)
                        for t in range(2):
                            sp.wait_ge(h3_out[t], 32 * B + 16)

                    @block.tensor
                    def _(pe):
                        pe.matmul(l_ps[0:NC, 0:P], hits[:, 0], ones[:], start=True, stop=True).then_inc(q["csum3"], 1)
                        pe.wait_ge(q["csel3"], 1)
                        for half in range(2):
                            pe.matmul(f_ps[:, half, :], csel[:], hit_rows[:, 512 * half:512 * half + 512], start=True,
                                      stop=True).then_inc(q["mask_full"], 1)
                        pe.wait_ge(q["p3sc"], 1)
                        for half in range(2):
                            wait(pe, q["cT3"], half)
                            for c in range(4):
                                h0 = P * (4 * half + c)
                                mm = pe.transpose(t_ps[:, P * c:P * c + P], hrow[:, h0:h0 + P], ident[:])
                            mm.then_inc(q["p3c"], 1)
                        pe.wait_ge(q["wm_done"], 2)

                        def turn2(b, i):
                            if not row(b):
                                return
                            if i % 2 == 0:
                                pe.wait_ge(ls2.xn, T * b + i // 2 + 1)
                            if i >= 2:
                                pe.wait_ge(q["n_lo"], 8 * b + i - 1)
                            else:
                                wait(pe, q["sig"], 16 * b)
                            for c in range(4):
                                h0 = P * (4 * (i % 2) + c)
                                mm = pe.transpose(s_ps[:, i % 2, P * c:P * c + P], xn2[:, i // 2, h0:h0 + P], ident[:])
                            mm.then_inc(q["n_full"], 1)

                        def ffn(b, u, a, z):
                            if not row(b):
                                return
                            t, half = u // 2, u % 2
                            if a == 0:
                                if half == 0:
                                    pe.wait_ge(fxT_in[t % 2], 32 * b + 16 * (t // 2) + 16)
                                wait(pe, q["x2_done"], 8 * b + u - 1)
                            for n in range(a, z):
                                c, (xp, wp) = n // 3, ((0, 0), (0, 1), (1, 0))[n % 3]
                                mm = pe.matmul(f_ps[:, half, :], fxT[:, t % 2, xp, c, :], wm[:, wp, c, 512 * half:512 * half + 512],
                                               start=(n == 0), stop=(n == 23))
                            if z == 24:
                                mm.then_inc(q["f_full"], 1)

                        def scores_b(b, hd):
                            if not row(b):
                                return
                            if hd == 0:
                                pe.wait_ge(q["n_lo"], 8 * b + 8)
                            for c in range(T):
                                wait(pe, q["sig"], 16 * b + 4 * hd + c - 1)
                                for i in range(6):
                                    d, (xp, yp) = 2 * hd + i // 3, ((0, 0), (0, 1), (1, 0))[i % 3]
                                    mm = pe.matmul(s_ps[:, c % 2, P * c:S], xhT[:, xp, d, P * c:P * c + P], yT[:, yp, d, P * c:S],
                                                   start=(i == 0), stop=(i == 5))
                                mm.then_inc(q["s_full"], 1)

                        def turn3(b, t, half):
                            if not row(b):
                                return
                            if half == 0:
                                pe.wait_ge(ls3.xn, T * b + t + 1)
                            wait(pe, q["h_lo"], 8 * b + 2 * t + half if not isinstance(b, int) or b > 0 or t + half > 0 else 0)
                            for c in range(4):
                                h0 = P * (4 * half + c)
                                mm = pe.transpose(t_ps[:, P * c:P * c + P], xn3[:, t, h0:h0 + P], ident[:])
                            mm.then_inc(q["h_full"], 1)

                        def weighted_b(b, hd):
                            if not row(b):
                                return
                            pe.wait_ge(q["a_lo"], 16 * b + 4 * hd + 4)
                            if hd == 0:
                                pe.wait_ge(q["v_lo"], T * (b + 1))
                            for t in range(T):
                                if t % 2 == 0:
                                    wait(pe, q["x3_done"], 8 * b + 2 * hd - 1 + t // 2 if not isinstance(b, int) or b > 0 or hd > 0 else 0)
                                last = 3 * (t + 1) - 1
                                for n in range(last + 1):
                                    c, (ap_, vp) = n // 3, ((0, 0), (0, 1), (1, 0))[n % 3]
                                    mm = pe.matmul(pv_ps[:, t // 2, t % 2, :], ahl[:, ap_, c, P * t:P * t + P],
                                                   vv[:, vp, c, D * hd:D * hd + D], start=(n == 0), stop=(n == last))
                                if t % 2:
                                    mm.then_inc(q["pv_full"], 1)

                        def logits(b, t):
                            if not row(b):
                                return
                            pe.wait_ge(q["h_lo"], 8 * b + 2 * t + 2)
                            if t == 0 and isinstance(b, int):
                                wait(pe, q["lsub"], b)
                            for n in range(24):
                                c, (xp, wp) = n // 3, ((0, 0), (0, 1), (1, 0))[n % 3]
                                mm = pe.matmul(l_ps[:, NC * t:NC * t + NC], h3T[:, t % 2, xp, c, :], centT[:, wp, c, :],
                                               start=(n == 0), stop=(n == 23))
                            mm.then_inc(q["l_full"], 1)

                        def step(b, par):
                            for i in range(2 * T):
                                turn2(b, i)
                                ffn(b + 1, i // 2, 12 * (i % 2), 12 * (i % 2) + 12)
                            for hd in range(HEADS_B):
                                scores_b(b, hd)
                                turn3(b - 1, hd, 0)
                                ffn(b + 1, 4 + hd, 0, 24)
                                turn3(b - 1, hd, 1)
                                weighted_b(b, hd)
                                logits(b - 1, hd)

                        batch_rows(pe, step)

                    @block.scalar
                    def _(act):
                        def hi2(b, i):
                            if not row(b):
                                return
                            act.wait_ge(q["n_full"], 8 * b + i + 1)
                            if i == 0:
                                wait(act, q["s_full"], 16 * b)
                            t, c0 = i // 2, 4 * (i % 2)
                            nc.scalar.activation(xhT[:, 0, c0:c0 + 4, P * t:P * t + P], s_ps[:, i % 2].rearrange("p (c n) -> p c n", c=4),
                                                 ACT.Copy).then_inc(q["n_hi"], 1)
                            for c in range(4):
                                nc.scalar.activation(yT[:, 0, c0 + c, P * t:P * t + P], s_ps[:, i % 2, P * c:P * c + P], ACT.Copy,
                                                     scale=cq[:, c0 + c:c0 + c + 1]).then_inc(q["n_hi"], 1)

                        def hi_v(b, t):
                            if not row(b):
                                return
                            act.wait_ge(q["v32"], T * b + t + 1)
                            if t == 0:
                                wait(act, q["pv_full"], 8 * b)
                            nc.scalar.activation(vv[:, 0, t], hrow[:], ACT.Copy).then_inc(q["v_hi"], 1)

                        def sigmoids(b, hd):
                            if not row(b):
                                return
                            wait(act, q["a_lo"], 16 * b + 4 * hd)
                            for c in range(T):
                                act.wait_ge(q["s_full"], 16 * b + 4 * hd + c + 1)
                                nc.scalar.activation(a32[:, c, P * c:S], s_ps[:, c % 2, P * c:S], ACT.Sigmoid,
                                                     scale=sig_scale[:, 0:1]).then_inc(q["sig"], 1)

                        def hi_a(b, hd):
                            if not row(b):
                                return
                            wait(act, q["pv_full"], 8 * b + 2 * hd)
                            for c in range(T):
                                act.wait_ge(q["tri"], 16 * b + 4 * hd + c + 1)
                                nc.scalar.activation(ahl[:, 0, c, P * c:S], a32[:, c, P * c:S], ACT.Copy).then_inc(q["a_hi"], 1)

                        def hi3(b, t, half):
                            if not row(b):
                                return
                            act.wait_ge(q["h_full"], 8 * b + 2 * t + half + 1)
                            if half == 0:
                                act.wait_ge(h3_out[t % 2], 32 * b + 16 * (t // 2) + 16)
                            nc.scalar.activation(h3T[:, t % 2, 0, 4 * half:4 * half + 4, :], t_ps[:].rearrange("p (c n) -> p c n", c=4),
                                                 ACT.Copy).then_inc(q["h_hi"], 1)

                        def step(b, par):
                            for i in range(2 * T):
                                hi2(b, i)
                                if i % 2:
                                    hi_v(b, i // 2)
                            for hd in range(HEADS_B):
                                sigmoids(b, hd)
                                hi3(b - 1, hd, 0)
                                hi_a(b, hd)
                                hi3(b - 1, hd, 1)
                            if row(b - 1):
                                act.wait_ge(q["lsub"], b)
                                nc.scalar.activation(c4[:], c4[:], ACT.Exp, scale=cent_scale[:, 0:1]).then_inc(q["lexp"], 1)

                        act.wait_ge(q["cT3"], 2)
                        batch_rows(act, step)

                    @block.vector
                    def _(dve):
                        k = [0]

                        def chain(ins):
                            k[0] += 1
                            ins.then_inc(q["mask3"], 1)
                            dve.wait_ge(q["mask3"], k[0])

                        dve.wait_ge(q["csum3"], 1)
                        dve.tensor_scalar(csel[:], l_ps[0:NC, 0:P], 0.5, None, ALU.is_gt).then_inc(q["csel3"], 1)
                        dve.wait_ge(q["bind_in"], 64)
                        tmp = xn3[:, 0]
                        for w in (hrow[:], xn2[:, 0], vb[:]):
                            wh = w.rearrange("p (h d) -> p h d", h=HEADS_B)
                            chain(dve.tensor_reduce(alpha[:], wh, AX.X, ALU.add, apply_absolute_value=True))
                            chain(dve.tensor_scalar(alpha[:], alpha[:], 1.0 / D, None, ALU.mult))
                            chain(dve.tensor_scalar(tmp, w, 0.0, 2.0, ALU.is_ge, ALU.mult))
                            chain(dve.tensor_scalar(tmp, tmp, -1.0, None, ALU.add))
                            chain(dve.tensor_tensor(tmp.rearrange("p (h d) -> p h d", h=HEADS_B), tmp.rearrange("p (h d) -> p h d", h=HEADS_B),
                                                    alpha[:].unsqueeze(2).to_broadcast([P, HEADS_B, D]), ALU.mult))
                            chain(dve.tensor_tensor(tmp, tmp, w, ALU.subtract))
                            chain(dve.tensor_tensor(w, tmp, w, ALU.add))
                        chain(dve.tensor_tensor(hrow[:], hrow[:], xn2[:, 0], ALU.mult))
                        chain(dve.tensor_reduce(m3[:, 0:1], hrow[:], AX.X, ALU.max, apply_absolute_value=True))
                        chain(dve.tensor_reduce(m3[:, 1:2], vb[:], AX.X, ALU.max, apply_absolute_value=True))
                        scale_from_absmax(dve, m3[:], e3[:], s3[:], q["p3all"], 0)
                        chain(dve.tensor_scalar(sig_scale[:], e3[:, 0:1], 4.0 * float(D) ** -0.5, None, ALU.mult))
                        chain(dve.tensor_scalar(vb[:], vb[:], s3[:, 1:2], None, ALU.mult))
                        chain(dve.tensor_scalar(hrow[:], hrow[:], s3[:, 0:1], None, ALU.mult))
                        chain(dve.tensor_scalar(inv_f[:], qsel[:, 0], e_w[:, 2:3], None, ALU.mult))
                        chain(dve.memset(h4[:], 0.0))
                        dve.sem_inc(q["p3sc"], 1)
                        for half in range(2):
                            dve.wait_ge(q["mask_full"], half + 1)
                            chain(dve.tensor_copy(mask[:, 512 * half:512 * half + 512], f_ps[:, half, :]))
                        chain(dve.tensor_tensor(fbias[:], fbias[:], mask[:], ALU.mult))
                        dve.wait_ge(w_in3, 16)
                        for part in range(2):
                            dve.tensor_tensor(wm[:, part], wm[:, part], mask[:].unsqueeze(1).to_broadcast([P, C, H]),
                                              ALU.mult).then_inc(q["wm_done"], 1)
                        for half in range(2):
                            dve.wait_ge(q["p3c"], half + 1)
                            dve.tensor_copy(cq[:, 4 * half:4 * half + 4].unsqueeze(2), t_ps[:].rearrange("p (c n) -> p c n", c=4)[:, :, 0:1]).then_inc(q["cT3"], 1)
                        dve.wait_ge(q["cT3"], 2)

                        def bias_x1(b, par, t):
                            if not row(b):
                                return
                            dve.wait_ge(x1_in[t], 16 * (b + 1))
                            dve.scalar_tensor_tensor(out=x2[:, par, t], in0=fbias[:], scalar=qsel[:, 0, bass.ds(T * b + t, 1)],
                                                     in1=x2[:, par, t], op0=ALU.mult, op1=ALU.add).then_inc(q["xb3"], 1)
                            dve.wait_ge(q["xb3"], T * b + t + 1)

                        def residual(b, par, u):
                            if not row(b):
                                return
                            t, half = u // 2, u % 2
                            if half == 0:
                                bias_x1(b, par, t)
                            cols = slice(512 * half, 512 * half + 512)
                            dve.wait_ge(q["f_full"], 8 * b + u + 1)
                            dve.scalar_tensor_tensor(out=x2[:, par, t, cols], in0=f_ps[:, half, :], scalar=inv_f[:, bass.ds(T * b + t, 1)],
                                                     in1=x2[:, par, t, cols], op0=ALU.mult, op1=ALU.add).then_inc(q["x2_done"], 1)
                            if half:
                                dve.wait_ge(q["x2_done"], 8 * b + u + 1)

                        def lo2(b, i):
                            if not row(b):
                                return
                            t, c0 = i // 2, 4 * (i % 2)
                            dve.wait_ge(q["n_hi"], 5 * (8 * b + i + 1))
                            dve.tensor_tensor(xhT[:, 1, c0:c0 + 4, P * t:P * t + P], s_ps[:, i % 2].rearrange("p (c n) -> p c n", c=4),
                                              xhT[:, 0, c0:c0 + 4, P * t:P * t + P], ALU.subtract)
                            for c in range(4):
                                mm = dve.scalar_tensor_tensor(out=yT[:, 1, c0 + c, P * t:P * t + P], in0=s_ps[:, i % 2, P * c:P * c + P],
                                                              scalar=cq[:, c0 + c:c0 + c + 1], in1=yT[:, 0, c0 + c, P * t:P * t + P],
                                                              op0=ALU.mult, op1=ALU.subtract)
                            mm.then_inc(q["n_lo"], 1)

                        def lo3(b, t, half):
                            if not row(b):
                                return
                            dve.wait_ge(q["h_hi"], 8 * b + 2 * t + half + 1)
                            dve.tensor_tensor(h3T[:, t % 2, 1, 4 * half:4 * half + 4, :], t_ps[:].rearrange("p (c n) -> p c n", c=4),
                                              h3T[:, t % 2, 0, 4 * half:4 * half + 4, :], ALU.subtract).then_inc(q["h_lo"], 1)

                        def lo_a(b, hd):
                            if not row(b):
                                return
                            for c in range(T):
                                dve.wait_ge(q["a_hi"], 16 * b + 4 * hd + c + 1)
                                dve.tensor_tensor(ahl[:, 1, c, P * c:S], a32[:, c, P * c:S], ahl[:, 0, c, P * c:S],
                                                  ALU.subtract).then_inc(q["a_lo"], 1)

                        def add_b(b, par, hd):
                            if not row(b):
                                return
                            for i in range(2):
                                dve.wait_ge(q["pv_full"], 8 * b + 2 * hd + i + 1)
                                xs = x2[:, par, 2 * i:2 * i + 2, D * hd:D * hd + D]
                                dve.scalar_tensor_tensor(out=xs, in0=pv_ps[:, i], scalar=e3[:, 1:2], in1=xs,
                                                         op0=ALU.mult, op1=ALU.add).then_inc(q["x3_done"], 1)

                        def select(b):
                            if not row(b):
                                return
                            lg = l_ps[:, 0:T * NC].rearrange("p (t c) -> p t c", t=T)
                            dve.wait_ge(q["l_full"], T * b + T)
                            dve.tensor_reduce(cm[:], lg, AX.X, ALU.max).then_inc(q["lmax"], 1)
                            dve.wait_ge(q["lmax"], b + 1)
                            dve.tensor_tensor(c4[:], lg, cm[:].unsqueeze(2).to_broadcast([P, T, NC]), ALU.subtract).then_inc(q["lsub"], 1)
                            dve.wait_ge(q["lexp"], b + 1)
                            dve.tensor_reduce(cs[:], c4[:], AX.X, ALU.add).then_inc(q["lsum"], 1)
                            dve.wait_ge(q["lsum"], b + 1)
                            dve.tensor_scalar(cs[:], cs[:], HIT, None, ALU.mult).then_inc(q["lthr"], 1)
                            dve.wait_ge(q["lthr"], b + 1)
                            dve.tensor_tensor(h4[:, 0], c4[:], cs[:].unsqueeze(2).to_broadcast([P, T, NC]), ALU.is_gt).then_inc(q["lhit"], 1)
                            dve.wait_ge(q["lhit"], b + 1)
                            dve.tensor_reduce(qsel[:, 1, bass.ds(T * b, T)], h4[:, 0], AX.X, ALU.max)
                            dve.tensor_tensor(h4[:, 1], h4[:, 1], h4[:, 0], ALU.max).then_inc(q["lacc"], 1)

                        def step(b, par):
                            for i in range(2 * T):
                                if i % 2 == 0:
                                    ln3_stats(b, par, i // 2)
                                lo2(b, i)
                                if i % 2 == 0:
                                    norm3(b, par, i // 2)
                                    if i >= 2:
                                        residual(b + 1, 1 - par, i // 2 - 1)
                                    if i == 4:
                                        ln2_stats(b, par, 0)
                                    if i == 6:
                                        norm2(b, par, 0)
                            for hd in range(HEADS_B):
                                lo3(b - 1, hd, 0)
                                if hd == 0:
                                    residual(b + 1, 1 - par, 3)
                                    ln2_stats(b, par, 1)
                                lo_a(b, hd)
                                if hd % 2 == 0:
                                    norm2(b, par, 1 + hd // 2)
                                residual(b + 1, 1 - par, 4 + hd)
                                if hd % 2:
                                    ln2_stats(b, par, 2 + hd // 2)
                                lo3(b - 1, hd, 1)
                                add_b(b, par, hd)
                            norm2(b, par, 3)
                            select(b - 1)

                        def ln3_stats(b, par, t):
                            if row(b - 1):
                                dve.wait_ge(q["x3_done"], 8 * b)
                                if t >= 2:
                                    dve.wait_ge(ls3.xn, T * (b - 1) + t - 1)
                                hit_stats(dve, ls3, ln3, x2[:, 1 - par, t], T * (b - 1) + t, t % 2)

                        def norm3(b, par, t):
                            if row(b - 1):
                                hit_norm(dve, ls3, ln3, x2[:, 1 - par, t], xn3[:, t], T * (b - 1) + t, t % 2)

                        def norm2(b, par, t):
                            if row(b + 1):
                                wait(dve, q["v32"], T * b + t + 1)
                                hit_norm(dve, ls2, ln2, x2[:, 1 - par, t], xn2[:, t], T * (b + 1) + t, t % 2)

                        def ln2_stats(b, par, t):
                            if row(b + 1):
                                wait(dve, ls2.xn, T * (b + 1) + t - 1)
                                hit_stats(dve, ls2, ln2, x2[:, 1 - par, t], T * (b + 1) + t, t % 2)

                        batch_rows(dve, step)
                        dve.wait_ge(q["lacc"], B)
                        chain(dve.tensor_tensor(h4[:, 1, 0:2], h4[:, 1, 0:2], h4[:, 1, 2:4], ALU.max))
                        dve.tensor_tensor(hits[:, 1], h4[:, 1, 0], h4[:, 1, 1], ALU.max)

                    @block.gpsimd
                    def _(pool):
                        def rstd3(b, t):
                            if row(b - 1):
                                hit_rstd(pool, nc, ls3, ln3, mhalf, T * (b - 1) + t, t % 2)

                        def rstd2(b, t):
                            if row(b + 1):
                                hit_rstd(pool, nc, ls2, ln2, mhalf, T * (b + 1) + t, t % 2)

                        def values(b, t):
                            if not row(b):
                                return
                            pool.wait_ge(ls2.xn, T * b + t + 1)
                            wait(pool, q["v_lo"], T * b + t)
                            nc.gpsimd.tensor_tensor(hrow[:], xn2[:, t], vb[:], ALU.mult).then_inc(q["v32"], 1)

                        def lo_v(b, t):
                            if not row(b):
                                return
                            pool.wait_ge(q["v_hi"], T * b + t + 1)
                            nc.gpsimd.tensor_tensor(vv[:, 1, t], hrow[:], vv[:, 0, t], ALU.subtract).then_inc(q["v_lo"], 1)

                        def triangle(b, hd):
                            if not row(b):
                                return
                            for c in range(T):
                                wait_apart(pool, q["sig"], 16 * b + 4 * hd + c + 1)
                                diag = a32[:, c, P * c:P * c + P]
                                nc.gpsimd.affine_select(out=diag, in_=diag, compare_op=ALU.is_ge, fill=0.0, base=0,
                                                        pattern=[[1, P]], channel_multiplier=-1).then_inc(q["tri"], 1)

                        def step(b, par):
                            for i in range(2 * T):
                                if i % 2 == 0:
                                    rstd3(b, i // 2)
                                    if i:
                                        lo_v(b, i // 2 - 1)
                                else:
                                    values(b, i // 2)
                                if i == 5:
                                    rstd2(b, 0)
                            lo_v(b, T - 1)
                            for hd in range(HEADS_B):
                                triangle(b, hd)
                                if hd == 0:
                                    rstd2(b, 1)
                                if hd % 2:
                                    rstd2(b, 2 + hd // 2)

                        pool.wait_ge(q["cT3"], 2)
                        batch_rows(pool, step)

            end_phase()

            with ExitStack() as p4:
                wm = sb(p4, "wm4", [P, 2, C, H], F16)
                csel = sb(p4, "csel4", [NC, P], F16)
                mask = sb(p4, "mask4", [P, H], F16)
                inv_f = sb(p4, "inv_f4", [P, B * T])
                xT = sb(p4, "xT4", [P, T, 2, C, P], F16)
                x3 = sb(p4, "x34", [P, T, H])
                l_ps = ps(p4, "l_ps4", [P, 512])
                f_ps = ps(p4, "f_ps4", [P, 2, 2, 512])
                bias_in, csum4, csel4, mask_full, prep4, wm4, f_full, xb4, x4 = (sem(n) for n in (
                    "bias_in4", "csum4", "csel4", "mask_full4", "prep4", "wm_done4", "f_full4", "xb4", "x4_done"))
                w_in4 = sem("w_in4")
                x_in4 = [sem(f"x_in4_{t}") for t in range(T)]
                x_out4 = [sem(f"x_out4_{t}") for t in range(T)]

                def rows4(eng, step):
                    for t in range(T):
                        step(0, t)
                    if B > 1:
                        with eng.Fori(1, B) as b:
                            for t in range(T):
                                step(b, t)

                with nc.Block() as block:
                    @block.sync
                    def _(sp):
                        sp.dma_start(wm[:], wT_d).then_inc(w_in4, 16)
                        sp.dma_start(fbias[:], fb.partition_broadcast(P)).then_inc(bias_in, 16)

                        def step(b, t):
                            wait(sp, x_out4[t], 16 * b)
                            sp.dma_start(xT[:, t], xT3_d[T * b + t]).then_inc(x_in4[t], 16)
                            sp.dma_start(x3[:, t], x3_d[T * b + t]).then_inc(x_in4[t], 16)

                        rows4(sp, step)
                        for t in range(T):
                            sp.wait_ge(x_out4[t], 16 * B)

                    @block.tensor
                    def _(pe):
                        pe.matmul(l_ps[0:NC, 0:P], hits[:, 1], ones[:], start=True, stop=True).then_inc(csum4, 1)
                        pe.wait_ge(csel4, 1)
                        for half in range(2):
                            pe.matmul(f_ps[:, 0, half, :], csel[:], hit_rows[:, 512 * half:512 * half + 512], start=True,
                                      stop=True).then_inc(mask_full, 1)
                        pe.wait_ge(wm4, 2)

                        def step(b, t):
                            pe.wait_ge(x_in4[t], 32 * (b + 1))
                            for half in range(2):
                                wait(pe, x4, 8 * b + 2 * t + half - 3)
                                for n in range(24):
                                    c, (xp, wp) = n // 3, ((0, 0), (0, 1), (1, 0))[n % 3]
                                    mm = pe.matmul(f_ps[:, t % 2, half, :], xT[:, t, xp, c, :], wm[:, wp, c, 512 * half:512 * half + 512],
                                                   start=(n == 0), stop=(n == 23))
                                mm.then_inc(f_full, 1)

                        rows4(pe, step)

                    @block.scalar
                    def _(act):
                        def step(b, t):
                            act.wait_ge(x4, 8 * b + 2 * t + 2)
                            act.dma_start(out_t[T * b + t], x3[:, t]).then_inc(x_out4[t], 16)

                        rows4(act, step)

                    @block.vector
                    def _(dve):
                        dve.wait_ge(csum4, 1)
                        dve.tensor_scalar(csel[:], l_ps[0:NC, 0:P], 0.5, None, ALU.is_gt).then_inc(csel4, 1)
                        dve.tensor_scalar(inv_f[:], qsel[:, 1], e_w[:, 2:3], None, ALU.mult).then_inc(prep4, 1)
                        for half in range(2):
                            dve.wait_ge(mask_full, half + 1)
                            dve.tensor_copy(mask[:, 512 * half:512 * half + 512], f_ps[:, 0, half, :]).then_inc(prep4, 1)
                        dve.wait_ge(prep4, 3)
                        dve.wait_ge(w_in4, 16)
                        for part in range(2):
                            dve.tensor_tensor(wm[:, part], wm[:, part], mask[:].unsqueeze(1).to_broadcast([P, C, H]),
                                              ALU.mult).then_inc(wm4, 1)
                        dve.wait_ge(bias_in, 16)
                        dve.tensor_tensor(fbias[:], fbias[:], mask[:], ALU.mult).then_inc(prep4, 1)
                        dve.wait_ge(prep4, 4)

                        def step(b, t):
                            dve.wait_ge(x_in4[t], 32 * (b + 1))
                            dve.scalar_tensor_tensor(out=x3[:, t], in0=fbias[:], scalar=qsel[:, 1, bass.ds(T * b + t, 1)],
                                                     in1=x3[:, t], op0=ALU.mult, op1=ALU.add).then_inc(xb4, 1)
                            dve.wait_ge(xb4, T * b + t + 1)
                            for half in range(2):
                                cols = slice(512 * half, 512 * half + 512)
                                dve.wait_ge(f_full, 8 * b + 2 * t + half + 1)
                                dve.scalar_tensor_tensor(out=x3[:, t, cols], in0=f_ps[:, t % 2, half, :],
                                                         scalar=inv_f[:, bass.ds(T * b + t, 1)], in1=x3[:, t, cols],
                                                         op0=ALU.mult, op1=ALU.add).then_inc(x4, 1)

                        rows4(dve, step)


_INS = ['L0_attn_a_x', 'L0_attn_a_attn_qkvw', 'L0_attn_a_attn_qkvb', 'L0_attn_a_attn_ow', 'L0_attn_a_attn_ob',
        'L0_attn_b_bv_q', 'L0_attn_b_bv_k', 'L0_attn_b_bv_v', 'L0_ffn_weight', 'L0_ffn_bias', 'L0_ffn_centroids',
        'L0_ffn_assignments']


def kernel(**inputs):
    import numpy as _np
    import concourse.bacc as _bacc
    from concourse import mybir as _mybir
    from concourse.bass_utils import run_bass_kernel_spmd as _run

    nc = _bacc.Bacc("TRN2", target_bir_lowering=False, num_devices=1)
    arrays, args = {}, []
    for name in _INS:
        a = _np.ascontiguousarray(inputs[name])
        arrays[f"in_{name}_dram"] = a
        args.append(nc.dram_tensor(f"in_{name}_dram", a.shape, _mybir.dt.from_np(a.dtype), kind="ExternalInput").ap())
    shape = inputs['L0_attn_a_x'].shape
    args.append(nc.dram_tensor("out_0_dram", shape, _mybir.dt.float32, kind="ExternalOutput").ap())
    hybrid_layer(nc, *args)
    r = _run(nc, [arrays], core_ids=[0])
    return r.results[0]["out_0_dram"]
```
